# Optimizing a Trainium2 kernel written in Bass

```python
import numpy as np
import jax
import jax.numpy as jnp

def _softmax(x, axis=-1):
    return jax.nn.softmax(x, axis=axis)

def _gelu(x):
    return jax.nn.gelu(x, approximate=True)

def _silu(x):
    return jax.nn.silu(x)

def _sigmoid(x):
    return jax.nn.sigmoid(x)

def _layernorm(x, axis=-1, eps=1e-05):
    m = jnp.mean(x, axis=axis, keepdims=True)
    v = jnp.var(x, axis=axis, keepdims=True)
    return (x - m) / jnp.sqrt(v + eps)

def _scatter_add(tgt, idx, src, axis=0):
    return tgt.at[idx].add(src)

def _segment_sum(src, seg, n):
    return jax.ops.segment_sum(src, seg, n)
kernel_name = 'mk_prb_d1_jaxref_r8_0f8b53'

def setup_inputs(seed: int=0):
    np.random.seed(seed)
    _w = jnp.asarray

    def _L0_attn_setup():
        import jax, jax.numpy as jnp
        import numpy as np
        D_MODEL = 128
        N_HEADS = 16
        HEAD_DIM = D_MODEL // N_HEADS
        KV_LATENT = 32
        LN_EPS = 1e-05

        def apply_rope(x):
            b, h, t, d = x.shape
            half = d // 2
            pos = jnp.arange(t, dtype=x.dtype)[:, None]
            inv_freq = 1.0 / 10000.0 ** (jnp.arange(half, dtype=x.dtype) / half)
            angles = pos * inv_freq[None, :]
            sin = jnp.sin(angles)[None, None]
            cos = jnp.cos(angles)[None, None]
            x1, x2 = (x[..., :half], x[..., half:])
            return jnp.concatenate([x1 * cos - x2 * sin, x1 * sin + x2 * cos], axis=-1)
        key = jax.random.key(seed)
        ks = jax.random.split(key, 6)
        d, L = (D_MODEL, KV_LATENT)
        s = 1.0 / np.sqrt(d)
        sl = 1.0 / np.sqrt(L)
        return {'x': jax.random.normal(ks[0], (2, 256, d), dtype=jnp.float32), 'W_q': jax.random.uniform(ks[1], (d, d), jnp.float32, -s, s), 'W_dkv': jax.random.uniform(ks[2], (d, L), jnp.float32, -s, s), 'W_uk': jax.random.uniform(ks[3], (L, d), jnp.float32, -sl, sl), 'W_uv': jax.random.uniform(ks[4], (L, d), jnp.float32, -sl, sl), 'W_o': jax.random.uniform(ks[5], (d, d), jnp.float32, -s, s), 'ln_gamma': jnp.ones((L,), jnp.float32), 'ln_beta': jnp.zeros((L,), jnp.float32)}
    _L0_attn_in = _L0_attn_setup()

    def _L0_ffn_setup():
        import jax, jax.numpy as jnp
        import numpy as np
        B, S, D, F, E = (4, 256, 128, 512, 8)
        key = jax.random.key(seed)
        ks = jax.random.split(key, 7)
        s1 = 1.0 / np.sqrt(D)
        s2 = 1.0 / np.sqrt(F)
        x = jax.random.normal(ks[0], (B, S, D), dtype=jnp.float32)
        W1 = jax.random.uniform(ks[1], (E, D, F), jnp.float32, -s1, s1)
        b1 = jax.random.uniform(ks[2], (E, F), jnp.float32, -s1, s1)
        W2 = jax.random.uniform(ks[3], (E, F, D), jnp.float32, -s2, s2)
        b2 = jax.random.uniform(ks[4], (E, D), jnp.float32, -s2, s2)
        Wr = jax.random.uniform(ks[5], (D, E), jnp.float32, -s1, s1)
        br = jax.random.uniform(ks[6], (E,), jnp.float32, -s1, s1)
        return {'x': x, 'W1': W1, 'b1': b1, 'W2': W2, 'b2': b2, 'Wr': Wr, 'br': br}
    _L0_ffn_in = _L0_ffn_setup()
    _d = {'L0_attn_x': _L0_attn_in['x'], 'L0_attn_W_q': _L0_attn_in['W_q'], 'L0_attn_W_dkv': _L0_attn_in['W_dkv'], 'L0_attn_W_uk': _L0_attn_in['W_uk'], 'L0_attn_W_uv': _L0_attn_in['W_uv'], 'L0_attn_W_o': _L0_attn_in['W_o'], 'L0_attn_ln_gamma': _L0_attn_in['ln_gamma'], 'L0_attn_ln_beta': _L0_attn_in['ln_beta'], 'L0_ffn_W1': _L0_ffn_in['W1'], 'L0_ffn_b1': _L0_ffn_in['b1'], 'L0_ffn_W2': _L0_ffn_in['W2'], 'L0_ffn_b2': _L0_ffn_in['b2'], 'L0_ffn_Wr': _L0_ffn_in['Wr'], 'L0_ffn_br': _L0_ffn_in['br']}
    _x0 = _d['L0_attn_x']
    _d['L0_attn_x'] = jax.random.normal(jax.random.fold_in(jax.random.key(seed), 1), (8, 256, 128), dtype=_x0.dtype)
    del _x0
    return _d

def reference(L0_attn_x, L0_attn_W_q, L0_attn_W_dkv, L0_attn_W_uk, L0_attn_W_uv, L0_attn_W_o, L0_attn_ln_gamma, L0_attn_ln_beta, L0_ffn_W1, L0_ffn_b1, L0_ffn_W2, L0_ffn_b2, L0_ffn_Wr, L0_ffn_br):

    def _L0_attn_ref(x, W_q, W_dkv, W_uk, W_uv, W_o, ln_gamma, ln_beta):
        import jax, jax.numpy as jnp
        import numpy as np
        D_MODEL = 128
        N_HEADS = 16
        HEAD_DIM = D_MODEL // N_HEADS
        KV_LATENT = 32
        LN_EPS = 1e-05

        def apply_rope(x):
            b, h, t, d = x.shape
            half = d // 2
            pos = jnp.arange(t, dtype=x.dtype)[:, None]
            inv_freq = 1.0 / 10000.0 ** (jnp.arange(half, dtype=x.dtype) / half)
            angles = pos * inv_freq[None, :]
            sin = jnp.sin(angles)[None, None]
            cos = jnp.cos(angles)[None, None]
            x1, x2 = (x[..., :half], x[..., half:])
            return jnp.concatenate([x1 * cos - x2 * sin, x1 * sin + x2 * cos], axis=-1)
        b, t, _ = x.shape
        q = (x @ W_q).reshape(b, t, N_HEADS, HEAD_DIM).transpose(0, 2, 1, 3)
        lat = x @ W_dkv
        mu = jnp.mean(lat, axis=-1, keepdims=True)
        var = jnp.mean(jnp.square(lat - mu), axis=-1, keepdims=True)
        lat = (lat - mu) * jax.lax.rsqrt(var + LN_EPS) * ln_gamma + ln_beta
        k = (lat @ W_uk).reshape(b, t, N_HEADS, HEAD_DIM).transpose(0, 2, 1, 3)
        v = (lat @ W_uv).reshape(b, t, N_HEADS, HEAD_DIM).transpose(0, 2, 1, 3)
        q = apply_rope(q)
        k = apply_rope(k)
        scores = jnp.einsum('bhqd,bhkd->bhqk', q, k) / jnp.sqrt(jnp.float32(HEAD_DIM))
        causal = jnp.tril(jnp.ones((t, t), dtype=bool))
        scores = jnp.where(causal[None, None], scores, -jnp.inf)
        attn = jax.nn.softmax(scores, axis=-1)
        out = jnp.einsum('bhqk,bhkd->bhqd', attn, v)
        out = out.transpose(0, 2, 1, 3).reshape(b, t, D_MODEL)
        return out @ W_o

    def _L0_ffn_ref(x, W1, b1, W2, b2, Wr, br):
        import jax, jax.numpy as jnp
        import numpy as np
        B, S, D, F, E = (4, 256, 128, 512, 8)
        b, s, d = x.shape
        e = Wr.shape[1]
        logits = x @ Wr + br
        idx = jnp.argmax(logits, axis=-1)
        probs = jax.nn.softmax(logits, axis=-1)
        gates = jnp.take_along_axis(probs, idx[..., None], axis=-1)[..., 0]
        xf = x.reshape(-1, d)
        idxf = idx.reshape(-1)
        gf = gates.reshape(-1)
        out = jnp.zeros_like(xf)
        for ei in range(e):
            h = jax.nn.gelu(xf @ W1[ei] + b1[ei], approximate=False)
            y = h @ W2[ei] + b2[ei]
            mask = (idxf == ei).astype(xf.dtype)
            out = out + y * (gf * mask)[:, None]
        return out.reshape(b, s, d)
    x = L0_attn_x
    xn = _layernorm(x, axis=-1)
    x = x + _L0_attn_ref(xn, L0_attn_W_q, L0_attn_W_dkv, L0_attn_W_uk, L0_attn_W_uv, L0_attn_W_o, L0_attn_ln_gamma, L0_attn_ln_beta) + _L0_ffn_ref(xn, L0_ffn_W1, L0_ffn_b1, L0_ffn_W2, L0_ffn_b2, L0_ffn_Wr, L0_ffn_br)
    return x

_drawn_inputs = setup_inputs


def setup_inputs(seed=0):
    import zlib

    import numpy as np

    out = dict(_drawn_inputs(seed))
    spreads = {'L0_attn_ln_gamma': (1.0, 0.6), 'L0_attn_ln_beta': (0.0, 0.1)}
    factors = {'L0_ffn_b1': 8.0, 'L0_ffn_b2': 8.0, 'L0_ffn_br': 3.771}
    for name, (base, spread) in spreads.items():
        noise = np.random.default_rng([zlib.crc32(name.encode()), seed]).standard_normal(out[name].shape)
        drawn = base * np.exp(spread * noise) if base else spread * noise
        out[name] = jnp.asarray(drawn.astype(out[name].dtype))
    for name, factor in factors.items():
        out[name] = (out[name] * factor).astype(out[name].dtype)
    return out
```

```python
from contextlib import ExitStack

import concourse.bass as bass
from concourse import mybir

F32 = mybir.dt.float32
BF16 = mybir.dt.bfloat16
I32 = mybir.dt.int32
ALU = mybir.AluOpType
ACT = mybir.ActivationFunctionType
AX = mybir.AxisListType

P = 128
B, S, D = 8, 256, 128
H, HD = 16, 8
L = 32
E, F = 8, 512
EPS = 1e-5
TILES = B * S // P
TPB = S // P
FC = F // P
SLOT_TILES = TILES + E - 1
G = 4
GROUPS = H // G
UNITS = B * GROUPS
PARTS = 6
ROWS = PARTS * HD
SH = ROWS + 2
QP = D + L + E
HW = 64
CH = 2 * TPB * G * HW
VW = 2 * G * HD
STW = G * (S + P)
NEG = -1.0e30


def layer_program(nc, x, W_q, W_dkv, W_uk, W_uv, W_o, ln_gamma, ln_beta, W1, b1, W2, b2, Wr, br, cos_t, sin_t, out):
    ctx = ExitStack()
    with ctx:
        def sb(name, shape, dt=F32):
            return ctx.enter_context(nc.sbuf_tensor(name, shape, dt))

        def sem(name):
            return ctx.enter_context(nc.semaphore(name))

        x_sb = sb("x_sb", [P, TILES, D])
        w_in = sb("w_in", [P, QP])
        w_kv = sb("w_kv", [P, 2 * D])
        w_o = sb("w_o", [P, 2, D])
        w1 = sb("w1", [P, E * F])
        w2 = sb("w2", [P, E * FC * D])
        b1_all = sb("b1_all", [P, E * F])
        b2_all = sb("b2_all", [P, E * D])
        gamma = sb("gamma", [P, L])
        beta = sb("beta", [P, L])
        br_all = sb("br_all", [P, E])
        cos_sb = sb("cos_sb", [P, TPB * G * HD])
        sin_sb = sb("sin_sb", [P, TPB * G * HD])
        ident = sb("ident", [P, P])
        ident_b = sb("ident_b", [P, P], BF16)
        before = sb("before", [P, P], BF16)
        ones_b = sb("ones_b", [P, P], BF16)
        causal_neg = sb("causal_neg", [P, P], BF16)
        tick = sb("tick", [P, 2])
        zeros = sb("zeros", [P, 4 * D])
        rank_of_e = sb("rank_of_e", [P, E])
        mult128 = sb("mult128", [P, TILES])
        tile_no = sb("tile_no", [P, SLOT_TILES])

        xn = sb("xn", [P, TILES, D])
        xnT = sb("xnT", [P, TILES * P])
        work = sb("work", [P, TILES * D])
        rope = sb("rope", [P, TILES * D])
        qk_raw = sb("qk_raw", [P, 2, TILES * D])
        low = sb("low", [P, TILES, L + E])
        latn = sb("latn", [P, TILES * L])
        latT = sb("latT", [P, 4, P])
        st = sb("st", [P, 12, TILES])
        rt = sb("rt", [P, 12, TILES * E])
        onehot_b = sb("onehot_b", [P, TILES * E], BF16)
        nte = sb("nte", [P, 6, E])
        cmp = sb("cmp", [P, SLOT_TILES * E])
        slot_f = sb("slot_f", [P, TILES])
        slot = sb("slot", [P, TILES], I32)
        expert_f = sb("expert_f", [P, SLOT_TILES])
        expert = sb("expert", [P, SLOT_TILES], I32)
        gate = sb("gate", [P, TILES])
        gsum = sb("gsum", [P, TILES])
        lshift = sb("lshift", [P, TILES * E])
        lexp = sb("lexp", [P, TILES * E])

        xs = [sb(f"xs{i}", [P, D]) for i in range(2)]
        xsT = [sb(f"xsT{i}", [P, P]) for i in range(2)]
        pre = [xnT[:, i * F:(i + 1) * F] for i in range(2)]
        hid = [xnT[:, (2 + i) * F:(3 + i) * F] for i in range(2)]
        hidT = [work[:, i * F:(i + 1) * F] for i in range(2)]
        y_sb = [sb(f"y_sb{i}", [P, D]) for i in range(2)]
        acc = xn

        stage = sb("stage", [P, UNITS * CH], BF16)
        stg = [b1_all[:, g * CH // 2:(g + 1) * CH // 2].bitcast(BF16) for g in range(GROUPS)]
        stk = [work[:, g * 2 * S:(g + 1) * 2 * S].bitcast(BF16).rearrange("p (k a t) -> p k a t", k=2, a=2)
               for g in range(GROUPS)]
        mx = sb("mx", [P, 2, 8])
        nm = sb("nm", [P, 2, 16], BF16)
        nmT = [rope[0:8, 4 * S + g * S // 2:4 * S + (g + 1) * S // 2].bitcast(BF16) for g in range(GROUPS)]
        probs = [qk_raw[:, i, 0:STW] for i in range(2)]
        v_all = sb("v_all", [P, TILES, D])
        VP = TPB * G * VW
        v_pad = [b1_all[:, GROUPS * CH // 2 + g * VP:GROUPS * CH // 2 + (g + 1) * VP] for g in range(GROUPS)]
        attn = rope[:, 0:2 * S]
        recip = rope[:, 2 * S:4 * S]
        o_sb = rope[:, 6 * S:6 * S + TPB * D]

        xs_dram = nc.dram_tensor("xs_dram", [SLOT_TILES * P, D], F32, kind="Internal").ap()
        ys_dram = nc.dram_tensor("ys_dram", [SLOT_TILES * P, D], F32, kind="Internal").ap()

        wide = ctx.enter_context(nc.psum_tensor("wide", [P, 3 * 512], F32))
        bank = [ctx.enter_context(nc.psum_tensor(f"bank{i}", [P, 512], F32)) for i in range(5)]
        p_xnT = [wide[:, 0:512], wide[:, 512:1024]]
        p_in = [bank[0], bank[1]]
        p_route = bank[2]
        p_latT = wide[:, 1024:1536]
        p_kv = [bank[3], bank[4], bank[0], bank[1]]
        p_pre = [wide[:, 0:512], wide[:, 512:1024]]
        p_hT = [wide[:, 1024:1536], bank[0][:, :]]
        p_xsT = bank[1]
        p_y = bank[2]
        p_st = wide
        p_sm = [bank[0], bank[1]]
        p_o = bank[2]
        p_stk = bank[3][:, :].bitcast(BF16)
        p_m = bank[4]
        p_mb = bank[4][:, :].bitcast(BF16)

        s_x = sem("s_x")
        s_win = sem("s_win")
        s_small = sem("s_small")
        s_w1 = sem("s_w1")
        s_w2 = sem("s_w2")
        s_bias = sem("s_bias")
        s_zero = sem("s_zero")
        s_init = sem("s_init")
        s_const = sem("s_const")
        s_pad = sem("s_pad")
        s_dve = sem("s_dve")
        s_act = sem("s_act")
        s_sq = sem("s_sq")
        s_var = sem("s_var")
        s_root = sem("s_root")
        s_xn = sem("s_xn")
        s_xnT = sem("s_xnT")
        s_xnTc = sem("s_xnTc")
        s_in = sem("s_in")
        s_qc = sem("s_qc")
        s_lowc = sem("s_lowc")
        s_onehot = sem("s_onehot")
        s_rank = sem("s_rank")
        s_slot = sem("s_slot")
        s_expert = sem("s_expert")
        s_latvar = sem("s_latvar")
        s_latroot = sem("s_latroot")
        s_latn = sem("s_latn")
        s_latT = sem("s_latT")
        s_latTc = sem("s_latTc")
        s_kv = sem("s_kv")
        s_kc = sem("s_kc")
        s_vc = sem("s_vc")
        s_rope = sem("s_rope")
        s_part = sem("s_part")
        s_stage = sem("s_stage")
        s_scat = sem("s_scat")
        xs_loaded = [sem(f"xs_loaded{i}") for i in range(2)]
        xsT_done = sem("xsT_done")
        xsT_copied = sem("xsT_copied")
        pre_done = sem("pre_done")
        bias_done = sem("bias_done")
        gelu_done = sem("gelu_done")
        hT_done = sem("hT_done")
        hT_copied = sem("hT_copied")
        y_done = sem("y_done")
        y_copied = sem("y_copied")
        y_stored = [sem(f"y_stored{i}") for i in range(2)]
        s_gath = sem("s_gath")
        s_lexp = sem("s_lexp")
        s_gate = sem("s_gate")
        s_acc = sem("s_acc")
        stg_loaded = [sem(f"stg_loaded{g}") for g in range(GROUPS)]
        stk_done = sem("stk_done")
        stk_copied = sem("stk_copied")
        sm_done = sem("sm_done")
        sm_read = sem("sm_read")
        sm_half = sem("sm_half")
        st_half = sem("st_half")
        nm_ready = sem("nm_ready")
        nmT_done = sem("nmT_done")
        nmT_copied = sem("nmT_copied")
        m_landed = [sem(f"m_landed{g}") for g in range(GROUPS)]
        st_done = sem("st_done")
        exp_done = sem("exp_done")
        mask_done = sem("mask_done")
        pv_done = sem("pv_done")
        attn_ready = sem("attn_ready")
        v_placed = sem("v_placed")
        proj_done = sem("proj_done")
        o_ready = sem("o_ready")
        s_neg = sem("s_neg")
        s_rec = sem("s_rec")
        s_out = sem("s_out")

        x_rows = x.rearrange("b t d -> (b t) d").rearrange("(j p) d -> p j d", p=P)
        out_rows = out.rearrange("b t d -> (b t) d").rearrange("(j p) d -> p j d", p=P)

        def mul(a, k):
            return a if k == 1 else a * k

        def grouped(ap):
            return ap.rearrange("p (u w d) -> p u w d", u=UNITS, d=HD)

        def product(qk, n):
            return stage[:, :].rearrange("p (u k w c) -> p k u w c", u=UNITS, k=2, c=HW)[
                :, qk, :, :, n * HD:(n + 1) * HD]

        def k_rows(g, c, a, tile, rows):
            return stk[g][64 * c:64 * c + rows, 1, a, tile * P:(tile + 1) * P]

        def q_rows(g, c, a, lo, hi, rows):
            return stk[g][64 * c:64 * c + rows, 0, a, lo:hi]

        def pad_columns(g, shift):
            step = VW + HD
            ap = [[E * F, P], [G * VW, TPB], [step, G], [1, HD]]
            return bass.AP(tensor=b1_all, offset=GROUPS * CH // 2 + g * VP + shift, ap=ap)

        block = ctx.enter_context(nc.Block())

        @block.sync
        def _(sp):
            for i in range(2):
                j = slice(i * TILES // 2, (i + 1) * TILES // 2)
                sp.dma_start(x_sb[:, j, :], x_rows[:, j, :]).then_inc(s_x, 16)
            sp.dma_start(w_in[:, 0:D], W_q).then_inc(s_win, 16)
            sp.dma_start(w_in[:, D:D + L], W_dkv).then_inc(s_win, 16)
            sp.dma_start(w_in[:, D + L:QP], Wr).then_inc(s_win, 16)
            for i in range(4):
                sp.dma_start(w_kv[L * i:L * (i + 1), 0:D], W_uk).then_inc(s_small, 16)
                sp.dma_start(w_kv[L * i:L * (i + 1), D:2 * D], W_uv).then_inc(s_small, 16)
            sp.dma_start(gamma[:, :], ln_gamma.partition_broadcast(P)).then_inc(s_small, 16)
            sp.dma_start(beta[:, :], ln_beta.partition_broadcast(P)).then_inc(s_small, 16)
            sp.dma_start(br_all[:, :], br.partition_broadcast(P)).then_inc(s_small, 16)
            sp.dma_start(cos_sb[:, :], cos_t).then_inc(s_small, 16)
            sp.dma_start(sin_sb[:, :], sin_t).then_inc(s_small, 16)
            sp.wait_ge(s_init, 8)
            for g in range(GROUPS):
                r = 64 * (g % 2)
                sp.dma_start(w_o[r:r + 32, g // 2, :], W_o[32 * g:32 * (g + 1), :]).then_inc(s_small, 16)
            sl = xs_dram.rearrange("(n p) d -> p n d", p=P)
            for n in range(0, SLOT_TILES, 4):
                k = min(4, SLOT_TILES - n)
                sp.dma_start(sl[:, n:n + k, :], zeros[:, 0:k * D].rearrange("p (k d) -> p k d", d=D)).then_inc(s_zero, 16)
            sp.dma_start(w1[:, :].rearrange("p (e f) -> p e f", e=E), W1.rearrange("e d f -> d e f")).then_inc(s_w1, 16)
            sp.dma_start(w2[:, :].rearrange("p (e c n) -> p e c n", e=E, c=FC),
                         W2.rearrange("e (c p) n -> p e c n", p=P)).then_inc(s_w2, 16)
            sp.dma_start(b1_all[:, :], b1.rearrange("e f -> (e f)").partition_broadcast(P)).then_inc(s_bias, 16)
            sp.dma_start(b2_all[:, :], b2.rearrange("e f -> (e f)").partition_broadcast(P)).then_inc(s_bias, 16)

            def load_slots(t, par):
                sp.dma_start(xs[par][:, :], xs_dram[bass.ds(t * P, P), :]).then_inc(xs_loaded[par], 16)

            def store_y(t, par):
                sp.wait_ge(y_copied, t + 1)
                sp.dma_start(ys_dram[bass.ds(t * P, P), :], y_sb[par][:, :]).then_inc(y_stored[par], 16)

            sp.wait_ge(s_scat, 16 * TILES)
            load_slots(0, 0)
            load_slots(1, 1)
            for t in (2, 3, 4):
                sp.wait_ge(xsT_done, t - 1)
                load_slots(t, t % 2)

            def expert_slot(t, par, load):
                if load:
                    sp.wait_ge(xsT_done, t + 4)
                    load_slots(t + 5, 1 - par)
                store_y(t, par)

            for t in (0, 1):
                expert_slot(t, t, True)
            with sp.Fori(2, 16, 2) as t:
                for par in range(2):
                    expert_slot(t + par, par, True)
            for t in range(16, SLOT_TILES):
                expert_slot(t, t % 2, t + 5 < SLOT_TILES)

            def load_unit(u, g):
                sp.dma_start(stg[g], stage[:, bass.ds(u * CH, CH)]).then_inc(stg_loaded[g], 16)

            def place_maxima(u, g):
                sp.wait_ge(nmT_copied, u + 1)
                for c in range(2):
                    for part in range(2):
                        lo = 4 * c + 2 * part
                        sp.dma_start(stk[g][64 * c + ROWS + part:64 * c + ROWS + part + 1, 0, :, :],
                                     nmT[g][lo:lo + 2, :]).then_inc(m_landed[g], 16)

            sp.wait_ge(s_stage, 1)
            sp.wait_ge(bias_done, SLOT_TILES)
            for u in range(GROUPS):
                load_unit(u, u)
            place_maxima(0, 0)

            def attention_unit(s, g, b, loads, maxima):
                if loads:
                    sp.wait_ge(stk_done, s + 1)
                    load_unit(s + GROUPS, g)
                if maxima:
                    place_maxima(s + 1, (g + 1) % GROUPS)
                if g == 3 and b is not None:
                    sp.wait_ge(o_ready, b)
                    sp.dma_start(out_rows[:, bass.ds((b - 1) * TPB, TPB), :],
                                 o_sb[:, :].rearrange("p (t d) -> p t d", t=TPB)).then_inc(s_out, 16)

            for g in range(GROUPS):
                attention_unit(g, g, None, True, True)
            with sp.Fori(1, B - 1) as b:
                for g in range(GROUPS):
                    attention_unit(b * GROUPS + g, g, b, True, True)
            for g in range(GROUPS):
                attention_unit((B - 1) * GROUPS + g, g, B - 1, False, g < 3)
            sp.wait_ge(o_ready, B)
            sp.dma_start(out_rows[:, (B - 1) * TPB:, :],
                         o_sb[:, :].rearrange("p (t d) -> p t d", t=TPB)).then_inc(s_out, 16)
            sp.wait_ge(s_out, 16 * B)

        @block.gpsimd
        def _(pool):
            pool.memset(ident[:, :], 0.0).then_inc(s_init, 1)
            pool.memset(ident_b[:, :], 0.0).then_inc(s_init, 1)
            pool.memset(ones_b[:, :], 1.0).then_inc(s_init, 1)
            pool.memset(before[:, :], 1.0).then_inc(s_init, 1)
            pool.memset(causal_neg[:, :], 0.0).then_inc(s_init, 1)
            pool.memset(zeros[:, :], 0.0).then_inc(s_init, 1)
            pool.memset(tick[:, :], 0.0).then_inc(s_init, 1)
            pool.memset(w_o[:, :, :], 0.0).then_inc(s_init, 1)
            pool.wait_ge(s_init, 8)
            for m in (ident, ident_b):
                pool.affine_select(out=m[:, :], in_=m[:, :], compare_op=ALU.not_equal, fill=1.0, base=0,
                                   pattern=[[-1, P]], channel_multiplier=1).then_inc(s_const, 1)
            pool.affine_select(out=before[:, :], in_=before[:, :], compare_op=ALU.is_gt, fill=0.0, base=0,
                               pattern=[[1, P]], channel_multiplier=-1).then_inc(s_const, 1)
            pool.affine_select(out=causal_neg[:, :], in_=causal_neg[:, :], compare_op=ALU.is_ge, fill=NEG,
                               base=0, pattern=[[-1, P]], channel_multiplier=1).then_inc(s_const, 1)
            pool.iota(rank_of_e[:, :], pattern=[[-1, E]], base=E, channel_multiplier=0,
                      allow_small_or_imprecise_dtypes=True).then_inc(s_const, 1)
            pool.iota(mult128[:, :], pattern=[[P, TILES]], base=0, channel_multiplier=0,
                      allow_small_or_imprecise_dtypes=True).then_inc(s_const, 1)
            pool.iota(tile_no[:, :], pattern=[[1, SLOT_TILES]], base=0, channel_multiplier=0,
                      allow_small_or_imprecise_dtypes=True).then_inc(s_const, 1)
            mrows = stage[:, :].rearrange("p (u k w c) -> p k u w c", u=UNITS, k=2, c=HW)
            for qk, lo, hi, value in ((0, ROWS, HW, 0.0), (1, ROWS, SH, 1.0), (1, SH, HW, 0.0)):
                pool.memset(mrows[:, qk, :, :, lo:hi], value).then_inc(s_const, 1)

            pool.wait_ge(s_slot, 1)
            pool.wait_ge(s_xn, 1)
            pool.wait_ge(s_zero, 16 * ((SLOT_TILES + 3) // 4))
            for j in range(TILES):
                pool.indirect_dma_start(out=xs_dram, out_offset=bass.IndirectOffsetOnAxis(slot[:, j:j + 1], 0),
                                        in_=xn[:, j, :], in_offset=None).then_inc(s_scat, 16)

            pool.wait_ge(bias_done, SLOT_TILES)
            pool.memset(b1_all[:, GROUPS * CH // 2:GROUPS * CH // 2 + GROUPS * VP], 0.0).then_inc(s_pad, 1)
            pool.wait_ge(s_pad, 1)
            for g in range(GROUPS):
                pool.memset(pad_columns(g, G * HD), 1.0).then_inc(s_pad, 1)

            pool.wait_ge(y_stored[0], 16 * ((SLOT_TILES + 1) // 2))
            pool.wait_ge(y_stored[1], 16 * (SLOT_TILES // 2))
            for j in range(TILES):
                pool.indirect_dma_start(out=acc[:, j, :], out_offset=None, in_=ys_dram,
                                        in_offset=bass.IndirectOffsetOnAxis(slot[:, j:j + 1], 0)).then_inc(s_gath, 16)

            def mask_unit(s, par, first=False):
                pool.wait_ge(exp_done, s + 1)
                if not first:
                    pool.wait_ge(mask_done, s * 2)
                pool.tensor_tensor(tick[:, 1:2], tick[:, 0:1], tick[:, 0:1], ALU.add)
                early = probs[par][:, 0:G * S].rearrange("p (h q) -> p h q", h=G)[:, :, 0:P]
                late = probs[par][:, G * S:STW].rearrange("p (h q) -> p h q", h=G)
                for part in (early, late):
                    pool.affine_select(out=part, in_=part, compare_op=ALU.is_ge, fill=0.0, base=0,
                                       pattern=[[0, G], [1, P]], channel_multiplier=-1).then_inc(mask_done, 1)

            def place_values(u, g, b, first=False):
                if not first:
                    pool.wait_ge(pv_done, u - 3)
                src = v_all[:, bass.ds(b * TPB, TPB), g * G * HD:(g + 1) * G * HD].rearrange(
                    "p t (h d) -> p t h d", h=G)
                pool.tensor_copy(pad_columns(g, 0), src).then_inc(v_placed, 1)

            pool.wait_ge(s_vc, TILES)
            pool.wait_ge(s_pad, 1 + GROUPS)
            for u in range(2):
                place_values(u, u, 0, first=True)
            for s in range(GROUPS):
                mask_unit(s, s % 2, first=(s == 0))
                place_values(s + 2, (s + 2) % GROUPS, (s + 2) // GROUPS, first=(s < 2))
            pool.wait_ge(s_gath, 16 * TILES)
            pool.wait_ge(s_gate, 1)
            gt = gate[:, :].unsqueeze(2).to_broadcast([P, TILES, D])
            pool.tensor_tensor(acc[:, :, :], acc[:, :, :], gt, ALU.mult).then_inc(s_acc, 1)
            pool.wait_ge(s_acc, 1)
            pool.tensor_tensor(acc[:, :, :], acc[:, :, :], x_sb[:, :, :], ALU.add).then_inc(s_acc, 1)
            with pool.Fori(1, B - 1) as b:
                for g in range(GROUPS):
                    mask_unit(b * GROUPS + g, g % 2)
                    place_values(b * GROUPS + g + 2, (g + 2) % GROUPS, b + (g + 2) // GROUPS)
            for g in range(GROUPS):
                s = (B - 1) * GROUPS + g
                mask_unit(s, g % 2)
                if g < 2:
                    place_values(s + 2, g + 2, B - 1)

        @block.scalar
        def _(act):
            act.wait_ge(s_sq, 1)
            nc.scalar.activation(work[:, :], xn[:, :, :].rearrange("p j d -> p (j d)"), ACT.Square).then_inc(s_sq, 1)
            act.wait_ge(s_var, 1)
            nc.scalar.activation(st[:, 3, :], st[:, 2, :], ACT.Sqrt).then_inc(s_root, 1)
            for a in range(TILES // 4):
                act.wait_ge(s_xnT, a + 1)
                nc.scalar.activation(xnT[:, a * 512:(a + 1) * 512], p_xnT[a % 2], ACT.Copy).then_inc(s_xnTc, 1)
            for a in range(TILES // 2):
                act.wait_ge(s_in, a + 1)
                src = p_in[a % 2][:, :].rearrange("p (t w) -> p t w", t=2)[:, :, 0:D].rearrange(
                    "p t (g w) -> p g t w", g=GROUPS)
                dst = qk_raw[:, 0, a * S:(a + 1) * S].rearrange("p (g t w) -> p g t w", g=GROUPS, t=TPB)
                nc.scalar.activation(dst, src, ACT.Copy, scale=float(HD) ** -0.5).then_inc(s_qc, 1)
            act.wait_ge(s_latvar, 1)
            nc.scalar.activation(st[:, 8, :], st[:, 7, :], ACT.Sqrt).then_inc(s_latroot, 1)
            act.wait_ge(s_latT, 1)
            nc.scalar.activation(latT[:, :, :].rearrange("p a t -> p (a t)"), p_latT, ACT.Copy).then_inc(s_latTc, 1)
            for j in range(TILES):
                act.wait_ge(s_kv, j + 1)
                src = p_kv[j % 4][:, 0:D].rearrange("p (g w) -> p g w", g=GROUPS)
                dst = qk_raw[:, 1, :].rearrange("p (b g t w) -> p b t g w", b=B, g=GROUPS, t=TPB)[:, j // TPB, j % TPB]
                nc.scalar.activation(dst, src, ACT.Copy).then_inc(s_kc, 1)
            act.wait_ge(s_const, 10)
            for qk in range(2):
                second = 3 if qk == 0 else 1
                act.wait_ge(s_rope, 2 * qk + 1)
                nc.scalar.activation(product(qk, 0), grouped(rope[:, :]), ACT.Copy).then_inc(s_part, 1)
                act.wait_ge(s_rope, 2 * qk + 2)
                nc.scalar.activation(product(qk, second), grouped(rope[:, :]), ACT.Copy).then_inc(s_part, 1)

            def gelu_tile(t, par):
                act.wait_ge(bias_done, t + 1)
                nc.scalar.activation(hid[par], pre[par], ACT.Gelu).then_inc(gelu_done, 1)

            def expert_slot(t, par, gelu):
                act.wait_ge(hT_done, t + 1)
                nc.scalar.activation(hidT[par], p_hT[par], ACT.Copy).then_inc(hT_copied, 1)
                if gelu:
                    gelu_tile(t + 1, 1 - par)

            gelu_tile(0, 0)
            for t in (0, 1):
                expert_slot(t, t, True)
            with act.Fori(2, 20, 2) as t:
                for par in range(2):
                    expert_slot(t + par, par, True)
            for t in range(20, SLOT_TILES):
                expert_slot(t, t % 2, t + 1 < SLOT_TILES)

            nc.scalar.activation(lexp[:, :], lshift[:, :], ACT.Exp).then_inc(s_lexp, 1)

            def copy_stack(w, g):
                act.wait_ge(stk_done, w + 1)
                nc.scalar.activation(work[:, g * 2 * S:(g + 1) * 2 * S].bitcast(BF16), p_stk,
                                     ACT.Copy).then_inc(stk_copied, 1)

            for w in range(3):
                copy_stack(w, w)

            def attention_unit(s, g, b, stack):
                act.wait_ge(st_done, s + 1)
                nc.scalar.activation(probs[g % 2], p_st[:, :], ACT.Exp).then_inc(exp_done, 1)
                if stack:
                    copy_stack(s + 3, (g + 3) % GROUPS)

            for g in range(GROUPS):
                attention_unit(g, g, None, True)
            with act.Fori(1, B - 1) as b:
                for g in range(GROUPS):
                    attention_unit(b * GROUPS + g, g, b, True)
            for g in range(GROUPS):
                attention_unit((B - 1) * GROUPS + g, g, B - 1, g == 0)

        @block.vector
        def _(dve):
            v = nc.vector
            steps = [0]

            def step(ins):
                steps[0] += 1
                ins.then_inc(s_dve, 1)
                dve.wait_ge(s_dve, steps[0])

            def bc(ap, n):
                return ap.unsqueeze(2).to_broadcast([P, ap.shape[1], n])

            def inverse_root(mean_sq, n, root_sem, ask_sem, r):
                step(v.tensor_scalar(st[:, r, :], mean_sq, 1.0 / n, EPS, ALU.mult, ALU.add))
                v.reciprocal(st[:, r + 1, :], st[:, r, :]).then_inc(ask_sem, 1)
                dve.wait_ge(root_sem, 1)
                step(v.tensor_tensor(st[:, 9, :], st[:, r + 2, :], st[:, r + 2, :], ALU.mult))
                step(v.tensor_tensor(st[:, 10, :], st[:, 9, :], st[:, r, :], ALU.mult))
                step(v.tensor_scalar(st[:, 9, :], st[:, 10, :], -0.5, 1.5, ALU.mult, ALU.add))
                step(v.tensor_tensor(st[:, 11, :], st[:, r + 2, :], st[:, 9, :], ALU.mult))

            dve.wait_ge(s_x, 32)
            step(v.tensor_reduce(st[:, 0, :], x_sb[:, :, :], AX.X, ALU.add))
            step(v.tensor_scalar(st[:, 4, :], st[:, 0, :], 1.0 / D, None, ALU.mult))
            v.tensor_tensor(xn[:, :, :], x_sb[:, :, :], bc(st[:, 4, :], D), ALU.subtract).then_inc(s_sq, 1)
            dve.wait_ge(s_sq, 2)
            step(v.tensor_reduce(st[:, 0, :], work[:, :].rearrange("p (j d) -> p j d", d=D), AX.X, ALU.add))
            inverse_root(st[:, 0, :], D, s_root, s_var, 1)
            v.tensor_tensor(xn[:, :, :], xn[:, :, :], bc(st[:, 11, :], D), ALU.mult).then_inc(s_xn, 1)

            for a in range(TILES // 2):
                dve.wait_ge(s_in, a + 1)
                src = p_in[a % 2][:, :].rearrange("p (t w) -> p t w", t=2)[:, :, D:QP]
                dve.wait_ge(s_qc, a + 1)
                v.tensor_copy(low[:, 2 * a:2 * a + 2, :], src).then_inc(s_lowc, 1)

            def e3(k):
                return rt[:, k, :].rearrange("p (j e) -> p j e", e=E)

            dve.wait_ge(s_small, 16 * 17)
            dve.wait_ge(s_lowc, TILES // 2)
            dve.wait_ge(s_const, 10)
            row_e = rank_of_e[:, :].unsqueeze(1).to_broadcast([P, TILES, E])
            step(v.tensor_tensor(e3(0), low[:, :, L:L + E], br_all[:, :].unsqueeze(1).to_broadcast([P, TILES, E]), ALU.add))
            step(v.tensor_reduce(st[:, 0, :], e3(0), AX.X, ALU.max))
            step(v.tensor_tensor(e3(1), e3(0), bc(st[:, 0, :], E), ALU.is_equal))
            step(v.tensor_tensor(lshift[:, :].rearrange("p (j e) -> p j e", e=E), e3(0), bc(st[:, 0, :], E), ALU.subtract))
            step(v.tensor_tensor(e3(2), e3(1), row_e, ALU.mult))
            step(v.tensor_reduce(st[:, 1, :], e3(2), AX.X, ALU.max))
            step(v.tensor_tensor(e3(3), row_e, bc(st[:, 1, :], E), ALU.is_equal))
            v.tensor_copy(onehot_b[:, :], rt[:, 3, :]).then_inc(s_onehot, 1)
            dve.wait_ge(s_rank, 1)
            step(v.tensor_copy(rt[:, 4, :], p_route[:, TILES * E:2 * TILES * E]))
            src = 4
            for k, dst in ((1, 5), (2, 6), (4, 5), (8, 6)):
                step(v.tensor_copy(rt[:, dst, 0:k * E], rt[:, src, 0:k * E]))
                step(v.tensor_tensor(rt[:, dst, k * E:], rt[:, src, k * E:], rt[:, src, 0:(TILES - k) * E], ALU.add))
                src = dst
            count = rt[:, 6, (TILES - 1) * E:TILES * E]
            c3 = cmp[:, 0:E * TILES].rearrange("p (e k) -> p e k", k=TILES)
            step(v.tensor_tensor(c3, bc(count, TILES), mult128[:, :].unsqueeze(1).to_broadcast([P, E, TILES]), ALU.is_gt))
            step(v.tensor_reduce(nte[:, 0, :], c3, AX.X, ALU.add))
            src = 0
            for k, dst in ((1, 1), (2, 2), (4, 1)):
                step(v.tensor_copy(nte[:, dst, 0:k], nte[:, src, 0:k]))
                step(v.tensor_tensor(nte[:, dst, k:], nte[:, src, k:], nte[:, src, 0:E - k], ALU.add))
                src = dst
            step(v.tensor_tensor(nte[:, 3, :], nte[:, 1, :], nte[:, 0, :], ALU.subtract))
            step(v.tensor_scalar(nte[:, 4, :], nte[:, 3, :], float(P), None, ALU.mult))
            step(v.tensor_tensor(rt[:, 7, :], rt[:, 6, :], rt[:, 4, :], ALU.subtract))
            step(v.tensor_tensor(rt[:, 8, :], rt[:, 7, :], p_route[:, 0:TILES * E], ALU.add))
            step(v.tensor_tensor(e3(9), e3(8), nte[:, 4, :].unsqueeze(1).to_broadcast([P, TILES, E]), ALU.add))
            step(v.tensor_tensor(e3(10), e3(9), e3(3), ALU.mult))
            step(v.tensor_reduce(slot_f[:, :], e3(10), AX.X, ALU.add))
            v.tensor_copy(slot[:, :], slot_f[:, :]).then_inc(s_slot, 1)
            x3 = cmp[:, :].rearrange("p (t e) -> p t e", e=E)
            step(v.tensor_tensor(x3, bc(tile_no[:, :], E), nte[:, 1, :].unsqueeze(1).to_broadcast([P, SLOT_TILES, E]), ALU.is_ge))
            step(v.tensor_reduce(expert_f[:, :], x3, AX.X, ALU.add))
            v.tensor_scalar(expert[:, :], expert_f[:, :], float(E - 1), None, ALU.min).then_inc(s_expert, 1)

            lat = low[:, :, 0:L]
            l3 = latn[:, :].rearrange("p (j l) -> p j l", l=L)
            sq = work[:, 0:TILES * L].rearrange("p (j l) -> p j l", l=L)
            step(v.tensor_reduce(st[:, 0, :], lat, AX.X, ALU.add))
            step(v.tensor_scalar(st[:, 4, :], st[:, 0, :], 1.0 / L, None, ALU.mult))
            step(v.tensor_tensor(l3, lat, bc(st[:, 4, :], L), ALU.subtract))
            step(v.tensor_tensor(sq, l3, l3, ALU.mult))
            step(v.tensor_reduce(st[:, 0, :], sq, AX.X, ALU.add))
            inverse_root(st[:, 0, :], L, s_latroot, s_latvar, 6)
            step(v.tensor_tensor(l3, l3, bc(st[:, 11, :], L), ALU.mult))
            step(v.tensor_tensor(l3, l3, gamma[:, :].unsqueeze(1).to_broadcast([P, TILES, L]), ALU.mult))
            v.tensor_tensor(l3, l3, beta[:, :].unsqueeze(1).to_broadcast([P, TILES, L]), ALU.add).then_inc(s_latn, 1)

            for j in range(TILES):
                dve.wait_ge(s_kv, j + 1)
                dve.wait_ge(s_kc, j + 1)
                v.tensor_copy(v_all[:, j, :], p_kv[j % 4][:, D:2 * D]).then_inc(s_vc, 1)

            half = HD // 2
            W8 = TPB * G
            cos_b = cos_sb[:, :].unsqueeze(1).to_broadcast([P, UNITS, W8 * HD])
            sin_b = sin_sb[:, :].rearrange("p (w d) -> p w d", d=HD).unsqueeze(1).to_broadcast([P, UNITS, W8, HD])
            for qk in range(2):
                raw = qk_raw[:, qk, :]
                step(v.tensor_tensor(rope[:, :].rearrange("p (u w) -> p u w", u=UNITS),
                                     raw.rearrange("p (u w) -> p u w", u=UNITS), cos_b, ALU.mult))
                for o in range(2):
                    mine, other = slice(o * half, (o + 1) * half), slice((1 - o) * half, (2 - o) * half)
                    step(v.tensor_tensor(grouped(work[:, :])[:, :, :, mine], grouped(raw)[:, :, :, other],
                                         sin_b[:, :, :, mine], ALU.mult))
                v.tensor_tensor(rope[:, :], rope[:, :], work[:, :], ALU.add).then_inc(s_rope, 1)
                dve.wait_ge(s_part, 2 * qk + 1)
                v.tensor_tensor(grouped(rope[:, :]), grouped(rope[:, :]), product(qk, 0), ALU.subtract).then_inc(s_rope, 1)
                copies = ((1, 0), (2, 0)) if qk == 0 else ((3, 0), (5, 0))
                for to, of in copies:
                    step(v.tensor_copy(product(qk, to), product(qk, of)))
                dve.wait_ge(s_part, 2 * qk + 2)
                second, third = (3, 5) if qk == 0 else (1, 2)
                step(v.tensor_tensor(product(qk, third), grouped(rope[:, :]), product(qk, second), ALU.subtract))
                ins = v.tensor_copy(product(qk, 4), product(qk, second))
                if qk == 0:
                    step(ins)
                else:
                    ins.then_inc(s_stage, 1)

            dve.wait_ge(s_bias, 32)
            dve.wait_ge(s_expert, 1)

            def copy_xT(t, par):
                dve.wait_ge(xsT_done, t + 1)
                v.tensor_copy(xsT[par][:, :], p_xsT[:, 0:P]).then_inc(xsT_copied, 1)

            def add_bias(t, par, gelu_before):
                e = nc.vector.value_load(expert[0:1, bass.ds(t, 1)], min_val=0, max_val=E - 1)
                dve.wait_ge(pre_done, t + 1)
                if gelu_before:
                    dve.wait_ge(gelu_done, t - 1)
                v.tensor_tensor(pre[par], p_pre[par], b1_all[:, bass.ds(e * F, F)], ALU.add).then_inc(bias_done, 1)

            def finish_y(t, par, n_stored):
                e = nc.vector.value_load(expert[0:1, bass.ds(t, 1)], min_val=0, max_val=E - 1)
                dve.wait_ge(y_done, t + 1)
                if n_stored is not None:
                    dve.wait_ge(y_stored[par], n_stored)
                v.tensor_tensor(y_sb[par][:, :], p_y[:, 0:D], b2_all[:, bass.ds(e * D, D)], ALU.add).then_inc(y_copied, 1)

            for t in range(3):
                copy_xT(t, t % 2)
            add_bias(0, 0, False)
            add_bias(1, 1, False)
            for t in (0, 1):
                copy_xT(t + 3, 1 - t)
                add_bias(t + 2, t, True)
                finish_y(t, t, None)
            with dve.Fori(1, 10) as i:
                for par in range(2):
                    t = i * 2 + par
                    copy_xT(t + 3, 1 - par)
                    add_bias(t + 2, par, True)
                    finish_y(t, par, i * 16)
            for t in range(20, SLOT_TILES):
                if t + 3 < SLOT_TILES:
                    copy_xT(t + 3, 1 - t % 2)
                if t + 2 < SLOT_TILES:
                    add_bias(t + 2, t % 2, True)
                finish_y(t, t % 2, 16 * (t // 2))

            dve.wait_ge(s_lexp, 1)
            step(v.tensor_reduce(gsum[:, :], lexp[:, :].rearrange("p (j e) -> p j e", e=E), AX.X, ALU.add))
            v.reciprocal(gate[:, :], gsum[:, :]).then_inc(s_gate, 1)

            step(v.memset(rope[:, 0:4 * S], 0.0))

            def read_scores(u, par):
                mv = mx[:, par, :].rearrange("p (t c a) -> p t c a", t=2, c=2)
                t0 = p_sm[0][:, :].rearrange("p (w n) -> p w n", n=P)
                t1 = p_sm[1][:, :].rearrange("p (a n) -> p a n", n=S)
                for k, (dst, src) in enumerate(((mv[:, 1, 0, :], t1), (mx[:, par, 0:4], t0), (mv[:, 1, 1, :], t1))):
                    dve.wait_ge(sm_done, u * 3 + k + 1)
                    v.tensor_reduce(dst, src, AX.X, ALU.max).then_inc(sm_read, 1)
                nv = nm[:, par, :].rearrange("p (w r a) -> p w r a", r=2, a=2)
                m2 = mx[:, par, :].rearrange("p (w a) -> p w a", a=2)
                dve.wait_ge(sm_read, u * 3 + 3)
                v.tensor_scalar(nv[:, :, 0, :], m2, -1.0, None, ALU.mult).then_inc(s_neg, 1)
                dve.wait_ge(s_neg, u + 1)
                v.scalar_tensor_tensor(nv[:, :, 1, :], m2, -1.0, nv[:, :, 0, :], ALU.mult, ALU.subtract).then_inc(nm_ready, 1)

            def copy_maxima(u, g):
                dve.wait_ge(nmT_done, u + 1)
                v.tensor_copy(nmT[g], p_mb[0:8, 0:S]).then_inc(nmT_copied, 1)

            def normalise(b):
                dve.wait_ge(pv_done, b * GROUPS)
                for r in (0, 64):
                    v.reciprocal(recip[r:r + 32, :], p_o[r + 32:r + 64, :]).then_inc(s_rec, 1)
                dve.wait_ge(s_rec, b * 2)
                v.tensor_tensor(attn[0:96, :], p_o[0:96, :], recip[0:96, :], ALU.mult).then_inc(attn_ready, 1)

            def finish_rows(b, first):
                dve.wait_ge(proj_done, b)
                if not first:
                    dve.wait_ge(s_out, (b - 1) * 16)
                v.tensor_tensor(o_sb[:, :].rearrange("p (t d) -> p t d", t=TPB),
                                p_m[:, 0:TPB * D].rearrange("p (t d) -> p t d", t=TPB),
                                acc[:, bass.ds((b - 1) * TPB, TPB), :], ALU.add).then_inc(o_ready, 1)

            def attention_unit(s, g, b, scores, first=False):
                if g == 1 and b is not None:
                    normalise(b)
                if scores:
                    read_scores(s + 2, g % 2)
                if g == 2 and b is not None:
                    finish_rows(b, first)
                if scores:
                    copy_maxima(s + 2, (g + 2) % GROUPS)

            for u in range(2):
                read_scores(u, u)
                copy_maxima(u, u)
            for g in range(GROUPS):
                attention_unit(g, g, None, True)
            dve.wait_ge(s_acc, 2)
            for g in range(GROUPS):
                attention_unit(GROUPS + g, g, 1, True, True)
            with dve.Fori(2, B - 1) as b:
                for g in range(GROUPS):
                    attention_unit(b * GROUPS + g, g, b, True)
            for g in range(GROUPS):
                attention_unit((B - 1) * GROUPS + g, g, B - 1, g < 2)
            normalise(B)
            finish_rows(B, False)

        @block.tensor
        def _(pe):
            mm = nc.tensor.matmul
            tr = nc.tensor.transpose
            pe.wait_ge(s_const, 10)
            pe.wait_ge(s_xn, 1)
            for a in range(TILES // 4):
                if a >= 2:
                    pe.wait_ge(s_xnTc, a - 1)
                for k in range(4):
                    ins = tr(p_xnT[a % 2][:, k * P:(k + 1) * P], xn[:, 4 * a + k, :], ident[:, :])
                ins.then_inc(s_xnT, 1)
            pe.wait_ge(s_win, 48)
            for a in range(TILES // 2):
                pe.wait_ge(s_xnTc, a // 2 + 1)
                if a >= 2:
                    pe.wait_ge(s_qc, a - 1)
                    pe.wait_ge(s_lowc, a - 1)
                for t in range(2):
                    j = 2 * a + t
                    ins = mm(p_in[a % 2][:, t * 256:t * 256 + QP], xnT[:, j * P:(j + 1) * P], w_in[:, :], start=True, stop=True)
                ins.then_inc(s_in, 1)
            pe.wait_ge(s_onehot, 1)
            n = TILES * E
            mm(p_route[:, 0:n], before[:, :], onehot_b[:, :], start=True, stop=True)
            mm(p_route[:, n:2 * n], ones_b[:, :], onehot_b[:, :], start=True, stop=True).then_inc(s_rank, 1)
            pe.wait_ge(s_latn, 1)
            for a in range(4):
                ins = tr(p_latT[:, a * P:(a + 1) * P], latn[:, a * P:(a + 1) * P], ident[:, :])
            ins.then_inc(s_latT, 1)
            pe.wait_ge(s_latTc, 1)
            pe.wait_ge(s_small, 16 * 17)
            pe.wait_ge(s_qc, TILES // 2)
            for j in range(TILES):
                if j >= 4:
                    pe.wait_ge(s_vc, j - 3)
                r = slice(L * (j % 4), L * (j % 4 + 1))
                mm(p_kv[j % 4][:, 0:2 * D], latT[r, j // 4, :], w_kv[r, :], start=True, stop=True).then_inc(s_kv, 1)

            def rows_T(t, par, loaded, copied):
                pe.wait_ge(xs_loaded[par], loaded)
                if copied is not None:
                    pe.wait_ge(xsT_copied, copied)
                tr(p_xsT[:, 0:P], xs[par][:, :], ident[:, :]).then_inc(xsT_done, 1)

            def first_half(t, par, biased):
                e = nc.tensor.value_load(expert[0:1, bass.ds(t, 1)], min_val=0, max_val=E - 1)
                pe.wait_ge(xsT_copied, t + 1)
                if biased is not None:
                    pe.wait_ge(bias_done, biased)
                mm(p_pre[par], xsT[par][:, :], w1[:, bass.ds(e * F, F)], start=True, stop=True).then_inc(pre_done, 1)

            def hidden_T(t, par, copied):
                pe.wait_ge(gelu_done, t + 1)
                if copied is not None:
                    pe.wait_ge(hT_copied, copied)
                for c in range(FC):
                    ins = tr(p_hT[par][:, c * P:(c + 1) * P], hid[par][:, c * P:(c + 1) * P], ident[:, :])
                ins.then_inc(hT_done, 1)

            def second_half(t, par, copied):
                e = nc.tensor.value_load(expert[0:1, bass.ds(t, 1)], min_val=0, max_val=E - 1)
                pe.wait_ge(hT_copied, t + 1)
                if copied is not None:
                    pe.wait_ge(y_copied, copied)
                for c in range(FC):
                    ins = mm(p_y[:, 0:D], hidT[par][:, c * P:(c + 1) * P], w2[:, bass.ds(e * (FC * D) + c * D, D)],
                             start=(c == 0), stop=(c == FC - 1))
                ins.then_inc(y_done, 1)

            pe.wait_ge(s_expert, 1)
            pe.wait_ge(s_vc, TILES)
            rows_T(0, 0, 16, None)
            rows_T(1, 1, 16, 1)
            pe.wait_ge(s_w1, 16)
            first_half(0, 0, None)
            rows_T(2, 0, 32, 2)
            first_half(1, 1, None)
            pe.wait_ge(s_w2, 16)
            for t in (0, 1):
                hidden_T(t, t, None)
                rows_T(t + 3, 1 - t, 32 + 16 * t, t + 3)
                first_half(t + 2, t, t + 1)
                second_half(t, t, None if t == 0 else 1)
            with pe.Fori(1, 10) as i:
                for par in range(2):
                    t = i * 2 + par
                    hidden_T(t, par, t - 1)
                    rows_T(t + 3, 1 - par, i * 16 + 32 + 16 * par, t + 3)
                    first_half(t + 2, par, t + 1)
                    second_half(t, par, t)
            for t in range(20, SLOT_TILES):
                hidden_T(t, t % 2, t - 1)
                if t + 3 < SLOT_TILES:
                    rows_T(t + 3, (t + 3) % 2, 16 * ((t + 3) // 2 + 1), t + 3)
                if t + 2 < SLOT_TILES:
                    first_half(t + 2, t % 2, t + 1)
                second_half(t, t % 2, t)

            def stack(w, g, loaded, first=False):
                pe.wait_ge(stg_loaded[g], loaded)
                if not first:
                    pe.wait_ge(stk_copied, w)
                for qk in range(2):
                    for a in range(2):
                        for t in range(TPB):
                            lo = ((qk * TPB + t) * G + 2 * a) * HW
                            to = (qk * 4 + a * 2 + t) * P
                            ins = tr(p_stk[:, to:to + P], stg[g][:, lo:lo + 2 * HW], ident_b[:, :])
                ins.then_inc(stk_done, 1)


            def mask(bk):
                mm(bk, ident_b[:, :], causal_neg[:, :].unsqueeze(1).to_broadcast([P, bk.shape[1], P]),
                   start=True, stop=False, skip_group_check=True)

            def by_query_tile0(g, c):
                for a in range(2):
                    to = (2 * c + a) * P
                    ins = mm(p_sm[0][:, to:to + P], q_rows(g, c, a, 0, P, ROWS), k_rows(g, c, a, 0, ROWS),
                             start=False, stop=(c == 1 and a == 1), skip_group_check=True)
                return ins

            def by_query_tile1(g, c):
                mask(p_sm[1][:, :].rearrange("p (a n) -> p a n", a=2)[:, :, P:S])
                for a in range(2):
                    ins = mm(p_sm[1][:, a * S:(a + 1) * S], q_rows(g, c, a, P, S, ROWS),
                             stk[g][64 * c:64 * c + ROWS, 1, a, 0:S], start=False, stop=(a == 1), skip_group_check=True)
                ins.then_inc(sm_done, 1)

            def scores_by_query(u, g, first=False):
                pe.wait_ge(stk_copied, u + 1)
                if not first:
                    pe.wait_ge(sm_read, u * 3)
                mask(p_sm[0][:, :].rearrange("p (w n) -> p w n", w=G))
                by_query_tile0(g, 0).then_inc(sm_half, 1)
                by_query_tile1(g, 0)
                pe.wait_ge(sm_half, u + 1)
                by_query_tile0(g, 1).then_inc(sm_done, 1)

            def scores_by_query_rest(u, g):
                pe.wait_ge(sm_read, u * 3 + 1)
                by_query_tile1(g, 1)

            def scores_by_key(s, g, landed, first=False):
                pe.wait_ge(m_landed[g], landed)
                if not first:
                    pe.wait_ge(exp_done, s)
                for c in range(2):
                    for a in range(2):
                        to = (2 * c + a) * S
                        mm(p_st[:, to:to + S], k_rows(g, c, a, 0, SH), q_rows(g, c, a, 0, S, SH), start=True, stop=True)
                    if c == 1:
                        pe.wait_ge(st_half, s + 1)
                    for a in range(2):
                        to = G * S + (2 * c + a) * P
                        ins = mm(p_st[:, to:to + P], k_rows(g, c, a, 1, SH), q_rows(g, c, a, P, S, SH), start=True, stop=True)
                    ins.then_inc(st_done if c else st_half, 1)

            def weigh_values(s, g):
                pe.wait_ge(mask_done, s * 2 + 2)
                pe.wait_ge(v_placed, s + 1)
                r, q = 64 * (g % 2), S * (g // 2)
                for n in range(G):
                    h = 2 * (n % 2) + n // 2
                    mm(p_o[r:r + 64, q:q + S], v_pad[g][:, h * VW:(h + 1) * VW], probs[g % 2][:, n * S:(n + 1) * S],
                       start=(n == 0), stop=False)
                for n in range(G):
                    h = 2 * (n % 2) + n // 2
                    ins = mm(p_o[r:r + 64, q + P:q + S], v_pad[g][:, (G + h) * VW:(G + h + 1) * VW],
                             probs[g % 2][:, G * S + n * P:G * S + (n + 1) * P], start=False, stop=(n == G - 1))
                ins.then_inc(pv_done, 1)

            def maxima_T(u, par):
                pe.wait_ge(nm_ready, u + 1)
                for t in range(TPB):
                    ins = tr(p_mb[0:8, t * P:(t + 1) * P], nm[:, par, 8 * t:8 * t + 8], ident_b[:, :])
                ins.then_inc(nmT_done, 1)

            def project(b):
                pe.wait_ge(attn_ready, b)
                for t in range(TPB):
                    for i in range(2):
                        ins = mm(p_m[:, t * D:(t + 1) * D], attn[:, i * S + t * P:i * S + (t + 1) * P], w_o[:, i, :],
                                 start=(i == 0), stop=(i == 1))
                ins.then_inc(proj_done, 1)

            def attention_unit(s, g, b, more_stack, more_scores, peeled=False):
                scores_by_key(s, g, (b + 1) * 64, first=peeled and g == 0)
                if more_scores:
                    scores_by_query(s + 2, (g + 2) % GROUPS)
                if more_stack:
                    stack(s + 3, (g + 3) % GROUPS, (b + (2 if g > 0 else 1)) * 16)
                if more_scores:
                    scores_by_query_rest(s + 2, (g + 2) % GROUPS)
                if not peeled and g == 2:
                    pe.wait_ge(nmT_copied, s + 2)
                    project(b)
                if not (peeled and g == 0):
                    if g == 1 and not peeled:
                        pe.wait_ge(attn_ready, b)
                    weigh_values(s - 1, (g + 3) % GROUPS)
                if more_scores:
                    if g == 2 and not peeled:
                        pe.wait_ge(o_ready, b)
                    else:
                        pe.wait_ge(nmT_copied, s + 2)
                    maxima_T(s + 2, g % 2)

            pe.wait_ge(y_copied, SLOT_TILES)
            stack(0, 0, 16, first=True)
            stack(1, 1, 16)
            scores_by_query(0, 0, first=True)
            scores_by_query_rest(0, 0)
            maxima_T(0, 0)
            stack(2, 2, 16)
            scores_by_query(1, 1)
            scores_by_query_rest(1, 1)
            pe.wait_ge(nmT_copied, 1)
            maxima_T(1, 1)
            for g in range(GROUPS):
                attention_unit(g, g, 0, True, True, peeled=True)
            with pe.Fori(1, B - 1) as b:
                for g in range(GROUPS):
                    attention_unit(b * GROUPS + g, g, b, True, True)
            for g in range(GROUPS):
                attention_unit((B - 1) * GROUPS + g, g, B - 1, g == 0, g < 2)
            weigh_values(UNITS - 1, GROUPS - 1)
            pe.wait_ge(o_ready, B - 1)
            project(B)


_IN = ["x", "W_q", "W_dkv", "W_uk", "W_uv", "W_o", "ln_gamma", "ln_beta", "W1", "b1", "W2", "b2", "Wr", "br", "cos", "sin"]


def kernel(L0_attn_x, L0_attn_W_q, L0_attn_W_dkv, L0_attn_W_uk, L0_attn_W_uv, L0_attn_W_o, L0_attn_ln_gamma,
           L0_attn_ln_beta, L0_ffn_W1, L0_ffn_b1, L0_ffn_W2, L0_ffn_b2, L0_ffn_Wr, L0_ffn_br):
    import numpy as np
    import concourse.bacc as bacc
    from concourse.bass_utils import run_bass_kernel_spmd

    half = HD // 2
    inv_freq = (np.float32(1.0) / np.power(np.float32(10000.0), np.arange(half, dtype=np.float32) / np.float32(half))).astype(np.float32)
    angle = (np.arange(S, dtype=np.float32)[:, None] * inv_freq[None, :]).astype(np.float32)
    cos = np.concatenate([np.cos(angle)] * 2, axis=1).astype(np.float32)
    sin = np.concatenate([-np.sin(angle), np.sin(angle)], axis=1).astype(np.float32)

    def table(t):
        t = t.reshape(TPB, P, 1, HD).transpose(1, 0, 2, 3)
        return np.ascontiguousarray(np.broadcast_to(t, (P, TPB, G, HD)).reshape(P, TPB * G * HD))

    values = [L0_attn_x, L0_attn_W_q, L0_attn_W_dkv, L0_attn_W_uk, L0_attn_W_uv, L0_attn_W_o, L0_attn_ln_gamma,
              L0_attn_ln_beta, L0_ffn_W1, L0_ffn_b1, L0_ffn_W2, L0_ffn_b2, L0_ffn_Wr, L0_ffn_br, table(cos), table(sin)]
    nc = bacc.Bacc("TRN2", target_bir_lowering=False, num_devices=1)
    arrays, args = {}, []
    for name, value in zip(_IN, values):
        a = np.ascontiguousarray(value)
        arrays[f"in_{name}"] = a
        args.append(nc.dram_tensor(f"in_{name}", a.shape, mybir.dt.from_np(a.dtype), kind="ExternalInput").ap())
    out = nc.dram_tensor("out_rows", (B, S, D), F32, kind="ExternalOutput").ap()
    layer_program(nc, *args, out)
    r = run_bass_kernel_spmd(nc, [arrays], core_ids=[0])
    return r.results[0]["out_rows"]
```

```python
from contextlib import ExitStack

import concourse.bass as bass
from concourse import mybir

F32 = mybir.dt.float32
BF16 = mybir.dt.bfloat16
I32 = mybir.dt.int32
ALU = mybir.AluOpType
ACT = mybir.ActivationFunctionType
AX = mybir.AxisListType

P = 128
B, S, D = 8, 256, 128
H, HD = 16, 8
L = 32
E, F = 8, 512
EPS = 1e-5
TILES = B * S // P
TPB = S // P
FC = F // P
SLOT_TILES = TILES + E - 1
G = 4
GROUPS = H // G
UNITS = B * GROUPS
PARTS = 6
ROWS = PARTS * HD
SH = ROWS + 2
QP = D + L + E
HW = 64
CH = 2 * TPB * G * HW
VW = 32
STW = G * (S + P)
NEG = -1.0e30


def layer_program(nc, x, W_q, W_dkv, W_uk, W_uv, W_o, ln_gamma, ln_beta, W1, b1, W2, b2, Wr, br, cos_t, sin_t, out):
    ctx = ExitStack()
    with ctx:
        def sb(name, shape, dt=F32):
            return ctx.enter_context(nc.sbuf_tensor(name, shape, dt))

        def sem(name):
            return ctx.enter_context(nc.semaphore(name))

        x_sb = sb("x_sb", [P, TILES, D])
        w_in = sb("w_in", [P, QP])
        w_kv = sb("w_kv", [P, 2 * D])
        w_o = sb("w_o", [P, 2, D])
        w1 = sb("w1", [P, E * F])
        w2 = sb("w2", [P, E * FC * D])
        b1_all = sb("b1_all", [P, E * F])
        b2_all = sb("b2_all", [P, E * D])
        gamma = sb("gamma", [P, L])
        beta = sb("beta", [P, L])
        br_all = sb("br_all", [P, E])
        cos_sb = sb("cos_sb", [P, TPB * G * HD])
        sin_sb = sb("sin_sb", [P, TPB * G * HD])
        ident = sb("ident", [P, P])
        ident_b = sb("ident_b", [P, P], BF16)
        before = sb("before", [P, P], BF16)
        ones_b = sb("ones_b", [P, P], BF16)
        causal_neg = sb("causal_neg", [P, P], BF16)
        tick = sb("tick", [P, 2])
        zeros = sb("zeros", [P, 4 * D])
        rank_of_e = sb("rank_of_e", [P, E])
        mult128 = sb("mult128", [P, TILES])
        tile_no = sb("tile_no", [P, SLOT_TILES])

        xn = sb("xn", [P, TILES, D])
        xnT = sb("xnT", [P, TILES * P])
        work = sb("work", [P, TILES * D])
        rope = sb("rope", [P, TILES * D])
        qk_raw = sb("qk_raw", [P, 2, TILES * D])
        low = sb("low", [P, TILES, L + E])
        latn = sb("latn", [P, TILES * L])
        latT = sb("latT", [P, 4, P])
        st = sb("st", [P, 12, TILES])
        rt = sb("rt", [P, 12, TILES * E])
        onehot_b = sb("onehot_b", [P, TILES * E], BF16)
        nte = sb("nte", [P, 6, E])
        cmp = sb("cmp", [P, SLOT_TILES * E])
        slot_f = sb("slot_f", [P, TILES])
        slot = sb("slot", [P, TILES], I32)
        expert_f = sb("expert_f", [P, SLOT_TILES])
        expert = sb("expert", [P, SLOT_TILES], I32)
        gate = sb("gate", [P, TILES])
        gsum = sb("gsum", [P, TILES])
        lshift = sb("lshift", [P, TILES * E])
        lexp = sb("lexp", [P, TILES * E])

        xs = [sb(f"xs{i}", [P, D]) for i in range(2)]
        xsT = [sb(f"xsT{i}", [P, P]) for i in range(2)]
        pre = [xnT[:, i * F:(i + 1) * F] for i in range(2)]
        hid = [xnT[:, (2 + i) * F:(3 + i) * F] for i in range(2)]
        hidT = [work[:, i * F:(i + 1) * F] for i in range(2)]
        y_sb = [sb(f"y_sb{i}", [P, D]) for i in range(2)]
        acc = xn

        stage = sb("stage", [P, UNITS * CH], BF16)
        stk = [work[:, g * 2 * S:(g + 1) * 2 * S].bitcast(BF16).rearrange("p (k a t) -> p k a t", k=2, a=2)
               for g in range(GROUPS)]
        mx = sb("mx", [P, 2, 8])
        nm = sb("nm", [P, 2, 16], BF16)
        nmT = [rope[0:8, 4 * S + g * S // 2:4 * S + (g + 1) * S // 2].bitcast(BF16) for g in range(GROUPS)]
        probs = [qk_raw[:, i, 0:STW] for i in range(2)]
        v_all = sb("v_all", [P, TILES, D])
        VP = TPB * G * VW
        v_pad = [b1_all[:, g * VP:(g + 1) * VP] for g in range(GROUPS)]
        attn = rope[:, 0:2 * S]
        recip = rope[:, 2 * S:4 * S]
        o_sb = [rope[:, 6 * S + i * TPB * D:6 * S + (i + 1) * TPB * D] for i in range(2)]
        sums = qk_raw[:, 0, STW:]
        attn_last = qk_raw[:, 1, STW:]
        spare = low[:, :, :].rearrange("p j w -> p (j w)")
        recip_raw = spare[:, 0:2 * S]
        recip_last = latn[:, :]
        SEG = 2 * S // (P // 8)
        den = spare[:, 2 * S:2 * S + SEG]
        inv = spare[:, 2 * S + SEG:2 * S + 2 * SEG]

        xs_dram = nc.dram_tensor("xs_dram", [SLOT_TILES * P, D], F32, kind="Internal").ap()
        inv_dram = nc.dram_tensor("inv_dram", [8, 2 * S], F32, kind="Internal").ap()
        ys_dram = nc.dram_tensor("ys_dram", [SLOT_TILES * P, D], F32, kind="Internal").ap()

        wide = ctx.enter_context(nc.psum_tensor("wide", [P, 3 * 512], F32))
        bank = [ctx.enter_context(nc.psum_tensor(f"bank{i}", [P, 512], F32)) for i in range(5)]
        p_xnT = [wide[:, 0:512], wide[:, 512:1024]]
        p_in = [bank[0], bank[1]]
        p_route = bank[2]
        p_latT = wide[:, 1024:1536]
        p_kv = [bank[3], bank[4], bank[0], bank[1]]
        p_pre = [wide[:, 0:512], wide[:, 512:1024]]
        p_hT = [wide[:, 1024:1536], bank[0][:, :]]
        p_xsT = bank[1]
        p_y = bank[2]
        p_st = wide
        p_sm = [bank[0], bank[1]]
        p_o = bank[2]
        p_stk = bank[3][:, :].bitcast(BF16)
        p_m = bank[4]
        p_mb = bank[4][:, :].bitcast(BF16)

        s_x = sem("s_x")
        s_win = sem("s_win")
        s_small = sem("s_small")
        s_w1 = sem("s_w1")
        s_w2 = sem("s_w2")
        s_bias = sem("s_bias")
        s_zero = sem("s_zero")
        s_init = sem("s_init")
        s_const = sem("s_const")
        s_pad = sem("s_pad")
        s_dve = sem("s_dve")
        s_act = sem("s_act")
        s_sq = sem("s_sq")
        s_var = sem("s_var")
        s_root = sem("s_root")
        s_xn = sem("s_xn")
        s_xnT = sem("s_xnT")
        s_xnTc = sem("s_xnTc")
        s_in = sem("s_in")
        s_qc = sem("s_qc")
        s_lowc = sem("s_lowc")
        s_onehot = sem("s_onehot")
        s_rank = sem("s_rank")
        s_slot = sem("s_slot")
        s_expert = sem("s_expert")
        s_latvar = sem("s_latvar")
        s_latroot = sem("s_latroot")
        s_latn = sem("s_latn")
        s_latT = sem("s_latT")
        s_latTc = sem("s_latTc")
        s_kv = sem("s_kv")
        s_kc = sem("s_kc")
        s_vc = sem("s_vc")
        s_rope = sem("s_rope")
        s_part = sem("s_part")
        s_stage = sem("s_stage")
        s_scat = sem("s_scat")
        xs_loaded = [sem(f"xs_loaded{i}") for i in range(2)]
        xsT_done = sem("xsT_done")
        xsT_copied = sem("xsT_copied")
        pre_done = sem("pre_done")
        bias_done = sem("bias_done")
        gelu_done = sem("gelu_done")
        hT_done = sem("hT_done")
        hT_copied = sem("hT_copied")
        y_done = sem("y_done")
        y_copied = sem("y_copied")
        y_stored = [sem(f"y_stored{i}") for i in range(2)]
        s_gath = sem("s_gath")
        s_lexp = sem("s_lexp")
        s_gate = sem("s_gate")
        s_acc = sem("s_acc")
        stk_done = sem("stk_done")
        stk_copied = sem("stk_copied")
        sm_done = sem("sm_done")
        sm_read = sem("sm_read")
        sm_half = sem("sm_half")
        st_half = sem("st_half")
        nm_ready = sem("nm_ready")
        nmT_done = sem("nmT_done")
        nmT_copied = sem("nmT_copied")
        m_landed = [sem(f"m_landed{g}") for g in range(GROUPS)]
        st_done = sem("st_done")
        exp_done = sem("exp_done")
        mask_done = sem("mask_done")
        pv_done = sem("pv_done")
        attn_ready = sem("attn_ready")
        v_placed = sem("v_placed")
        proj_done = sem("proj_done")
        o_ready = sem("o_ready")
        s_neg = sem("s_neg")
        s_rec = sem("s_rec")
        sums_copied = sem("sums_copied")
        den_landed = sem("den_landed")
        inv_ready = sem("inv_ready")
        inv_stored = sem("inv_stored")
        inv_landed = sem("inv_landed")
        attn_zero = sem("attn_zero")
        half_ready = sem("half_ready")
        last_landed = sem("last_landed")
        s_out = sem("s_out")

        x_rows = x.rearrange("b t d -> (b t) d").rearrange("(j p) d -> p j d", p=P)
        out_rows = out.rearrange("b t d -> (b t) d").rearrange("(j p) d -> p j d", p=P)

        def mul(a, k):
            return a if k == 1 else a * k

        def grouped(ap):
            return ap.rearrange("p (u w d) -> p u w d", u=UNITS, d=HD)

        def product(qk, n):
            return stage[:, :].rearrange("p (u k w c) -> p k u w c", u=UNITS, k=2, c=HW)[
                :, qk, :, :, n * HD:(n + 1) * HD]

        def k_rows(g, c, a, tile, rows):
            return stk[g][64 * c:64 * c + rows, 1, a, tile * P:(tile + 1) * P]

        def q_rows(g, c, a, lo, hi, rows):
            return stk[g][64 * c:64 * c + rows, 0, a, lo:hi]

        def pad_columns(g, shift):
            ap = [[E * F, P], [G * VW, TPB], [2 * VW + HD, 2], [VW, 2], [1, HD]]
            return bass.AP(tensor=b1_all, offset=g * VP + shift, ap=ap)

        block = ctx.enter_context(nc.Block())

        @block.sync
        def _(sp):
            for i in range(2):
                j = slice(i * TILES // 2, (i + 1) * TILES // 2)
                sp.dma_start(x_sb[:, j, :], x_rows[:, j, :]).then_inc(s_x, 16)
            sp.dma_start(w_in[:, 0:D], W_q).then_inc(s_win, 16)
            sp.dma_start(w_in[:, D:D + L], W_dkv).then_inc(s_win, 16)
            sp.dma_start(w_in[:, D + L:QP], Wr).then_inc(s_win, 16)
            for i in range(4):
                sp.dma_start(w_kv[L * i:L * (i + 1), 0:D], W_uk).then_inc(s_small, 16)
                sp.dma_start(w_kv[L * i:L * (i + 1), D:2 * D], W_uv).then_inc(s_small, 16)
            sp.dma_start(gamma[:, :], ln_gamma.partition_broadcast(P)).then_inc(s_small, 16)
            sp.dma_start(beta[:, :], ln_beta.partition_broadcast(P)).then_inc(s_small, 16)
            sp.dma_start(br_all[:, :], br.partition_broadcast(P)).then_inc(s_small, 16)
            sp.dma_start(cos_sb[:, :], cos_t).then_inc(s_small, 16)
            sp.dma_start(sin_sb[:, :], sin_t).then_inc(s_small, 16)
            sp.wait_ge(s_init, 8)
            for g in range(GROUPS):
                for c in range(2):
                    r = 64 * (g % 2) + 32 * c
                    src = W_o.rearrange("(g a c d) n -> g c a d n", g=GROUPS, a=2, c=2)[g, c]
                    sp.dma_start(w_o[r:r + 2 * HD, g // 2, :], src).then_inc(s_small, 16)
            sl = xs_dram.rearrange("(n p) d -> p n d", p=P)
            for n in range(0, SLOT_TILES, 4):
                k = min(4, SLOT_TILES - n)
                sp.dma_start(sl[:, n:n + k, :], zeros[:, 0:k * D].rearrange("p (k d) -> p k d", d=D)).then_inc(s_zero, 16)
            sp.dma_start(w1[:, :].rearrange("p (e f) -> p e f", e=E), W1.rearrange("e d f -> d e f")).then_inc(s_w1, 16)
            sp.dma_start(w2[:, :].rearrange("p (e c n) -> p e c n", e=E, c=FC),
                         W2.rearrange("e (c p) n -> p e c n", p=P)).then_inc(s_w2, 16)
            sp.dma_start(b1_all[:, :], b1.rearrange("e f -> (e f)").partition_broadcast(P)).then_inc(s_bias, 16)
            sp.dma_start(b2_all[:, :], b2.rearrange("e f -> (e f)").partition_broadcast(P)).then_inc(s_bias, 16)

            def load_slots(t, par):
                sp.dma_start(xs[par][:, :], xs_dram[bass.ds(t * P, P), :]).then_inc(xs_loaded[par], 16)

            def store_y(t, par):
                sp.wait_ge(y_copied, t + 1)
                sp.dma_start(ys_dram[bass.ds(t * P, P), :], y_sb[par][:, :]).then_inc(y_stored[par], 16)

            sp.wait_ge(s_scat, 16 * TILES)
            load_slots(0, 0)
            load_slots(1, 1)
            for t in (2, 3, 4):
                sp.wait_ge(xsT_done, t - 1)
                load_slots(t, t % 2)

            def expert_slot(t, par, load):
                if load:
                    sp.wait_ge(xsT_done, t + 4)
                    load_slots(t + 5, 1 - par)
                store_y(t, par)

            for t in (0, 1):
                expert_slot(t, t, True)
            with sp.Fori(2, 16, 2) as t:
                for par in range(2):
                    expert_slot(t + par, par, True)
            for t in range(16, SLOT_TILES):
                expert_slot(t, t % 2, t + 5 < SLOT_TILES)

            def place_maxima(u, g):
                sp.wait_ge(nmT_copied, u + 1)
                for part in range(2):
                    sp.dma_start(stk[g][ROWS + part:P:64, 0, :, :], nmT[g][4 * part:4 * part + 4, :]).then_inc(m_landed[g], 16)

            for u in range(2):
                place_maxima(u, u)

            def spread_sums(n):
                sp.wait_ge(sums_copied, n)
                for i in range(2):
                    sp.dma_start(den[64 * i:64 * (i + 1), :], sums[(2 + i) * HD:P:32, :]).then_inc(den_landed, 16)

            def store_inverses(n):
                sp.wait_ge(inv_ready, n)
                sp.dma_start(inv_dram.rearrange("r (s k) -> (r s) k", k=SEG), inv).then_inc(inv_stored, 16)

            def load_inverses(n):
                sp.wait_ge(inv_stored, n * 16)
                for j in range(4):
                    src = inv_dram.rearrange("(a j) q -> j a q", j=4)[j].unsqueeze(1).to_broadcast([2, HD, 2 * S])
                    sp.dma_start(recip[32 * j:32 * j + 2 * HD, :], src).then_inc(inv_landed, 16)

            def store_rows(b):
                sp.wait_ge(o_ready, b + 1)
                sp.dma_start(out_rows[:, bass.ds(b * TPB, TPB), :],
                             o_sb[0].rearrange("p (t d) -> p t d", t=TPB)).then_inc(s_out, 16)

            def attention_unit(s, g, b, maxima, sums_too, rows_too):
                if maxima:
                    place_maxima(s + 2, (g + 2) % GROUPS)
                if sums_too and g == 1:
                    spread_sums(b)
                if sums_too and g == 2:
                    store_inverses(b)
                if sums_too and g == 3:
                    load_inverses(b)
                if rows_too and g == 3:
                    store_rows(b - 2)

            sp.wait_ge(attn_zero, 2)
            for g in range(GROUPS):
                attention_unit(g, g, 0, True, False, False)
            for g in range(GROUPS):
                attention_unit(GROUPS + g, g, 1, True, True, False)
            with sp.Fori(2, B - 1) as b:
                for g in range(GROUPS):
                    attention_unit(b * GROUPS + g, g, b, True, True, True)
            for g in range(GROUPS):
                attention_unit((B - 1) * GROUPS + g, g, B - 1, g < 2, True, True)
            for i in range(2):
                sp.wait_ge(s_rec, i + 1)
                for j in range(4):
                    r, q = 32 * j, slice(i * S, (i + 1) * S)
                    sp.dma_start(recip_last[r:r + 2 * HD, q], recip_raw[r + 2 * HD:r + 4 * HD, q]).then_inc(last_landed, 16)
                if i == 0:
                    store_rows(B - 2)
            sp.wait_ge(o_ready, B)
            sp.dma_start(out_rows[:, (B - 1) * TPB:, :],
                         o_sb[1].rearrange("p (t d) -> p t d", t=TPB)).then_inc(s_out, 16)
            sp.wait_ge(s_out, 16 * B)

        @block.gpsimd
        def _(pool):
            pool.memset(ident[:, :], 0.0).then_inc(s_init, 1)
            pool.memset(ident_b[:, :], 0.0).then_inc(s_init, 1)
            pool.memset(ones_b[:, :], 1.0).then_inc(s_init, 1)
            pool.memset(before[:, :], 1.0).then_inc(s_init, 1)
            pool.memset(causal_neg[:, :], 0.0).then_inc(s_init, 1)
            pool.memset(zeros[:, :], 0.0).then_inc(s_init, 1)
            pool.memset(tick[:, :], 0.0).then_inc(s_init, 1)
            pool.memset(w_o[:, :, :], 0.0).then_inc(s_init, 1)
            pool.wait_ge(s_init, 8)
            for m in (ident, ident_b):
                pool.affine_select(out=m[:, :], in_=m[:, :], compare_op=ALU.not_equal, fill=1.0, base=0,
                                   pattern=[[-1, P]], channel_multiplier=1).then_inc(s_const, 1)
            pool.affine_select(out=before[:, :], in_=before[:, :], compare_op=ALU.is_gt, fill=0.0, base=0,
                               pattern=[[1, P]], channel_multiplier=-1).then_inc(s_const, 1)
            pool.affine_select(out=causal_neg[:, :], in_=causal_neg[:, :], compare_op=ALU.is_ge, fill=NEG,
                               base=0, pattern=[[-1, P]], channel_multiplier=1).then_inc(s_const, 1)
            pool.iota(rank_of_e[:, :], pattern=[[-1, E]], base=E, channel_multiplier=0,
                      allow_small_or_imprecise_dtypes=True).then_inc(s_const, 1)
            pool.iota(mult128[:, :], pattern=[[P, TILES]], base=0, channel_multiplier=0,
                      allow_small_or_imprecise_dtypes=True).then_inc(s_const, 1)
            pool.iota(tile_no[:, :], pattern=[[1, SLOT_TILES]], base=0, channel_multiplier=0,
                      allow_small_or_imprecise_dtypes=True).then_inc(s_const, 1)
            mrows = stage[:, :].rearrange("p (u k w c) -> p k u w c", u=UNITS, k=2, c=HW)
            for qk, lo, hi, value in ((0, ROWS, HW, 0.0), (1, ROWS, SH, 1.0), (1, SH, HW, 0.0)):
                pool.memset(mrows[:, qk, :, :, lo:hi], value).then_inc(s_const, 1)

            pool.wait_ge(s_slot, 1)
            pool.wait_ge(s_xn, 1)
            pool.wait_ge(s_zero, 16 * ((SLOT_TILES + 3) // 4))
            for j in range(TILES):
                pool.indirect_dma_start(out=xs_dram, out_offset=bass.IndirectOffsetOnAxis(slot[:, j:j + 1], 0),
                                        in_=xn[:, j, :], in_offset=None).then_inc(s_scat, 16)

            pool.wait_ge(bias_done, SLOT_TILES)
            pool.memset(b1_all[:, 0:GROUPS * VP], 0.0).then_inc(s_pad, 1)
            pool.wait_ge(s_pad, 1)
            for g in range(GROUPS):
                pool.memset(pad_columns(g, 2 * HD), 1.0).then_inc(s_pad, 1)

            pool.wait_ge(y_stored[0], 16 * ((SLOT_TILES + 1) // 2))
            pool.wait_ge(y_stored[1], 16 * (SLOT_TILES // 2))
            for j in range(TILES):
                pool.indirect_dma_start(out=acc[:, j, :], out_offset=None, in_=ys_dram,
                                        in_offset=bass.IndirectOffsetOnAxis(slot[:, j:j + 1], 0)).then_inc(s_gath, 16)

            def mask_unit(s, par, first=False):
                pool.wait_ge(exp_done, s + 1)
                if not first:
                    pool.wait_ge(mask_done, s * 2)
                pool.tensor_tensor(tick[:, 1:2], tick[:, 0:1], tick[:, 0:1], ALU.add)
                early = probs[par][:, 0:G * S].rearrange("p (h q) -> p h q", h=G)[:, :, 0:P]
                late = probs[par][:, G * S:STW].rearrange("p (h q) -> p h q", h=G)
                for part in (early, late):
                    pool.affine_select(out=part, in_=part, compare_op=ALU.is_ge, fill=0.0, base=0,
                                       pattern=[[0, G], [1, P]], channel_multiplier=-1).then_inc(mask_done, 1)

            def place_values(u, g, b, first=False):
                if not first:
                    pool.wait_ge(pv_done, u - 3)
                src = v_all[:, bass.ds(b * TPB, TPB), g * G * HD:(g + 1) * G * HD].rearrange(
                    "p t (h d) -> p t h d", h=G)
                pool.tensor_copy(pad_columns(g, 0), src).then_inc(v_placed, 1)

            pool.wait_ge(s_vc, TILES)
            pool.wait_ge(s_pad, 1 + GROUPS)
            for u in range(2):
                place_values(u, u, 0, first=True)
            for s in range(GROUPS):
                mask_unit(s, s % 2, first=(s == 0))
                place_values(s + 2, (s + 2) % GROUPS, (s + 2) // GROUPS, first=(s < 2))
            pool.wait_ge(s_gath, 16 * TILES)
            pool.wait_ge(s_gate, 1)
            gt = gate[:, :].unsqueeze(2).to_broadcast([P, TILES, D])
            pool.tensor_tensor(acc[:, :, :], acc[:, :, :], gt, ALU.mult).then_inc(s_acc, 1)
            pool.wait_ge(s_acc, 1)
            pool.tensor_tensor(acc[:, :, :], acc[:, :, :], x_sb[:, :, :], ALU.add).then_inc(s_acc, 1)

            def normalise(n, first=False):
                pool.wait_ge(inv_landed, n * 64)
                if not first:
                    pool.wait_ge(proj_done, n - 1)
                pool.tensor_tensor(attn, sums, recip, ALU.mult).then_inc(attn_ready, 1)

            for g in range(GROUPS):
                mask_unit(GROUPS + g, g % 2)
                place_values(GROUPS + g + 2, (g + 2) % GROUPS, 1 + (g + 2) // GROUPS)
            pool.wait_ge(attn_zero, 1)
            normalise(1, first=True)
            with pool.Fori(2, B - 1) as b:
                for g in range(GROUPS):
                    mask_unit(b * GROUPS + g, g % 2)
                    place_values(b * GROUPS + g + 2, (g + 2) % GROUPS, b + (g + 2) // GROUPS)
                normalise(b)
            for g in range(GROUPS):
                s = (B - 1) * GROUPS + g
                mask_unit(s, g % 2)
                if g < 2:
                    place_values(s + 2, g + 2, B - 1)
            normalise(B - 1)

        @block.scalar
        def _(act):
            act.wait_ge(s_sq, 1)
            nc.scalar.activation(work[:, :], xn[:, :, :].rearrange("p j d -> p (j d)"), ACT.Square).then_inc(s_sq, 1)
            act.wait_ge(s_var, 1)
            nc.scalar.activation(st[:, 3, :], st[:, 2, :], ACT.Sqrt).then_inc(s_root, 1)
            for a in range(TILES // 4):
                act.wait_ge(s_xnT, a + 1)
                nc.scalar.activation(xnT[:, a * 512:(a + 1) * 512], p_xnT[a % 2], ACT.Copy).then_inc(s_xnTc, 1)
            for a in range(TILES // 2):
                act.wait_ge(s_in, a + 1)
                src = p_in[a % 2][:, :].rearrange("p (t w) -> p t w", t=2)[:, :, 0:D].rearrange(
                    "p t (g w) -> p g t w", g=GROUPS)
                dst = qk_raw[:, 0, a * S:(a + 1) * S].rearrange("p (g t w) -> p g t w", g=GROUPS, t=TPB)
                nc.scalar.activation(dst, src, ACT.Copy, scale=float(HD) ** -0.5).then_inc(s_qc, 1)
            act.wait_ge(s_latvar, 1)
            nc.scalar.activation(st[:, 8, :], st[:, 7, :], ACT.Sqrt).then_inc(s_latroot, 1)
            act.wait_ge(s_latT, 1)
            nc.scalar.activation(latT[:, :, :].rearrange("p a t -> p (a t)"), p_latT, ACT.Copy).then_inc(s_latTc, 1)
            for j in range(TILES):
                act.wait_ge(s_kv, j + 1)
                src = p_kv[j % 4][:, 0:D].rearrange("p (g w) -> p g w", g=GROUPS)
                dst = qk_raw[:, 1, :].rearrange("p (b g t w) -> p b t g w", b=B, g=GROUPS, t=TPB)[:, j // TPB, j % TPB]
                nc.scalar.activation(dst, src, ACT.Copy).then_inc(s_kc, 1)
            act.wait_ge(s_const, 10)
            for qk in range(2):
                second = 3 if qk == 0 else 1
                act.wait_ge(s_rope, 2 * qk + 1)
                nc.scalar.activation(product(qk, 0), grouped(rope[:, :]), ACT.Copy).then_inc(s_part, 1)
                act.wait_ge(s_rope, 2 * qk + 2)
                nc.scalar.activation(product(qk, second), grouped(rope[:, :]), ACT.Copy).then_inc(s_part, 1)

            def gelu_tile(t, par):
                act.wait_ge(bias_done, t + 1)
                nc.scalar.activation(hid[par], pre[par], ACT.Gelu).then_inc(gelu_done, 1)

            def expert_slot(t, par, gelu):
                act.wait_ge(hT_done, t + 1)
                nc.scalar.activation(hidT[par], p_hT[par], ACT.Copy).then_inc(hT_copied, 1)
                if gelu:
                    gelu_tile(t + 1, 1 - par)

            gelu_tile(0, 0)
            for t in (0, 1):
                expert_slot(t, t, True)
            with act.Fori(2, 20, 2) as t:
                for par in range(2):
                    expert_slot(t + par, par, True)
            for t in range(20, SLOT_TILES):
                expert_slot(t, t % 2, t + 1 < SLOT_TILES)

            nc.scalar.activation(lexp[:, :], lshift[:, :], ACT.Exp).then_inc(s_lexp, 1)

            def copy_stack(w, g):
                act.wait_ge(stk_done, w + 1)
                nc.scalar.activation(work[:, g * 2 * S:(g + 1) * 2 * S].bitcast(BF16), p_stk,
                                     ACT.Copy).then_inc(stk_copied, 1)

            for w in range(GROUPS):
                copy_stack(w, w)

            def copy_sums(n):
                act.wait_ge(pv_done, n * GROUPS)
                if not isinstance(n, int) or n > 1:
                    act.wait_ge(attn_ready, n - 1)
                nc.scalar.activation(sums, p_o[:, :], ACT.Copy).then_inc(sums_copied, 1)

            def attention_unit(s, g, b, stack):
                if g == 1 and b is not None:
                    copy_sums(b)
                act.wait_ge(st_done, s + 1)
                nc.scalar.activation(probs[g % 2], p_st[:, :], ACT.Exp).then_inc(exp_done, 1)
                if stack:
                    copy_stack(s + 4, g)

            for g in range(GROUPS):
                attention_unit(g, g, None, True)
            for g in range(GROUPS):
                attention_unit(GROUPS + g, g, 1, True)
            with act.Fori(2, B - 1) as b:
                for g in range(GROUPS):
                    attention_unit(b * GROUPS + g, g, b, True)
            for g in range(GROUPS):
                attention_unit((B - 1) * GROUPS + g, g, B - 1, False)

        @block.vector
        def _(dve):
            v = nc.vector
            steps = [0]

            def step(ins):
                steps[0] += 1
                ins.then_inc(s_dve, 1)
                dve.wait_ge(s_dve, steps[0])

            def bc(ap, n):
                return ap.unsqueeze(2).to_broadcast([P, ap.shape[1], n])

            def inverse_root(mean_sq, n, root_sem, ask_sem, r):
                step(v.tensor_scalar(st[:, r, :], mean_sq, 1.0 / n, EPS, ALU.mult, ALU.add))
                v.reciprocal(st[:, r + 1, :], st[:, r, :]).then_inc(ask_sem, 1)
                dve.wait_ge(root_sem, 1)
                step(v.tensor_tensor(st[:, 9, :], st[:, r + 2, :], st[:, r + 2, :], ALU.mult))
                step(v.tensor_tensor(st[:, 10, :], st[:, 9, :], st[:, r, :], ALU.mult))
                step(v.tensor_scalar(st[:, 9, :], st[:, 10, :], -0.5, 1.5, ALU.mult, ALU.add))
                step(v.tensor_tensor(st[:, 11, :], st[:, r + 2, :], st[:, 9, :], ALU.mult))

            dve.wait_ge(s_x, 32)
            step(v.tensor_reduce(st[:, 0, :], x_sb[:, :, :], AX.X, ALU.add))
            step(v.tensor_scalar(st[:, 4, :], st[:, 0, :], 1.0 / D, None, ALU.mult))
            v.tensor_tensor(xn[:, :, :], x_sb[:, :, :], bc(st[:, 4, :], D), ALU.subtract).then_inc(s_sq, 1)
            dve.wait_ge(s_sq, 2)
            step(v.tensor_reduce(st[:, 0, :], work[:, :].rearrange("p (j d) -> p j d", d=D), AX.X, ALU.add))
            inverse_root(st[:, 0, :], D, s_root, s_var, 1)
            v.tensor_tensor(xn[:, :, :], xn[:, :, :], bc(st[:, 11, :], D), ALU.mult).then_inc(s_xn, 1)

            for a in range(TILES // 2):
                dve.wait_ge(s_in, a + 1)
                src = p_in[a % 2][:, :].rearrange("p (t w) -> p t w", t=2)[:, :, D:QP]
                dve.wait_ge(s_qc, a + 1)
                v.tensor_copy(low[:, 2 * a:2 * a + 2, :], src).then_inc(s_lowc, 1)

            def e3(k):
                return rt[:, k, :].rearrange("p (j e) -> p j e", e=E)

            dve.wait_ge(s_small, 16 * 21)
            dve.wait_ge(s_lowc, TILES // 2)
            dve.wait_ge(s_const, 10)
            row_e = rank_of_e[:, :].unsqueeze(1).to_broadcast([P, TILES, E])
            step(v.tensor_tensor(e3(0), low[:, :, L:L + E], br_all[:, :].unsqueeze(1).to_broadcast([P, TILES, E]), ALU.add))
            step(v.tensor_reduce(st[:, 0, :], e3(0), AX.X, ALU.max))
            step(v.tensor_tensor(e3(1), e3(0), bc(st[:, 0, :], E), ALU.is_equal))
            step(v.tensor_tensor(lshift[:, :].rearrange("p (j e) -> p j e", e=E), e3(0), bc(st[:, 0, :], E), ALU.subtract))
            step(v.tensor_tensor(e3(2), e3(1), row_e, ALU.mult))
            step(v.tensor_reduce(st[:, 1, :], e3(2), AX.X, ALU.max))
            step(v.tensor_tensor(e3(3), row_e, bc(st[:, 1, :], E), ALU.is_equal))
            v.tensor_copy(onehot_b[:, :], rt[:, 3, :]).then_inc(s_onehot, 1)
            dve.wait_ge(s_rank, 1)
            step(v.tensor_copy(rt[:, 4, :], p_route[:, TILES * E:2 * TILES * E]))
            src = 4
            for k, dst in ((1, 5), (2, 6), (4, 5), (8, 6)):
                step(v.tensor_copy(rt[:, dst, 0:k * E], rt[:, src, 0:k * E]))
                step(v.tensor_tensor(rt[:, dst, k * E:], rt[:, src, k * E:], rt[:, src, 0:(TILES - k) * E], ALU.add))
                src = dst
            count = rt[:, 6, (TILES - 1) * E:TILES * E]
            c3 = cmp[:, 0:E * TILES].rearrange("p (e k) -> p e k", k=TILES)
            step(v.tensor_tensor(c3, bc(count, TILES), mult128[:, :].unsqueeze(1).to_broadcast([P, E, TILES]), ALU.is_gt))
            step(v.tensor_reduce(nte[:, 0, :], c3, AX.X, ALU.add))
            src = 0
            for k, dst in ((1, 1), (2, 2), (4, 1)):
                step(v.tensor_copy(nte[:, dst, 0:k], nte[:, src, 0:k]))
                step(v.tensor_tensor(nte[:, dst, k:], nte[:, src, k:], nte[:, src, 0:E - k], ALU.add))
                src = dst
            step(v.tensor_tensor(nte[:, 3, :], nte[:, 1, :], nte[:, 0, :], ALU.subtract))
            step(v.tensor_scalar(nte[:, 4, :], nte[:, 3, :], float(P), None, ALU.mult))
            step(v.tensor_tensor(rt[:, 7, :], rt[:, 6, :], rt[:, 4, :], ALU.subtract))
            step(v.tensor_tensor(rt[:, 8, :], rt[:, 7, :], p_route[:, 0:TILES * E], ALU.add))
            step(v.tensor_tensor(e3(9), e3(8), nte[:, 4, :].unsqueeze(1).to_broadcast([P, TILES, E]), ALU.add))
            step(v.tensor_tensor(e3(10), e3(9), e3(3), ALU.mult))
            step(v.tensor_reduce(slot_f[:, :], e3(10), AX.X, ALU.add))
            v.tensor_copy(slot[:, :], slot_f[:, :]).then_inc(s_slot, 1)
            x3 = cmp[:, :].rearrange("p (t e) -> p t e", e=E)
            step(v.tensor_tensor(x3, bc(tile_no[:, :], E), nte[:, 1, :].unsqueeze(1).to_broadcast([P, SLOT_TILES, E]), ALU.is_ge))
            step(v.tensor_reduce(expert_f[:, :], x3, AX.X, ALU.add))
            v.tensor_scalar(expert[:, :], expert_f[:, :], float(E - 1), None, ALU.min).then_inc(s_expert, 1)

            lat = low[:, :, 0:L]
            l3 = latn[:, :].rearrange("p (j l) -> p j l", l=L)
            sq = work[:, 0:TILES * L].rearrange("p (j l) -> p j l", l=L)
            step(v.tensor_reduce(st[:, 0, :], lat, AX.X, ALU.add))
            step(v.tensor_scalar(st[:, 4, :], st[:, 0, :], 1.0 / L, None, ALU.mult))
            step(v.tensor_tensor(l3, lat, bc(st[:, 4, :], L), ALU.subtract))
            step(v.tensor_tensor(sq, l3, l3, ALU.mult))
            step(v.tensor_reduce(st[:, 0, :], sq, AX.X, ALU.add))
            inverse_root(st[:, 0, :], L, s_latroot, s_latvar, 6)
            step(v.tensor_tensor(l3, l3, bc(st[:, 11, :], L), ALU.mult))
            step(v.tensor_tensor(l3, l3, gamma[:, :].unsqueeze(1).to_broadcast([P, TILES, L]), ALU.mult))
            v.tensor_tensor(l3, l3, beta[:, :].unsqueeze(1).to_broadcast([P, TILES, L]), ALU.add).then_inc(s_latn, 1)

            for j in range(TILES):
                dve.wait_ge(s_kv, j + 1)
                dve.wait_ge(s_kc, j + 1)
                v.tensor_copy(v_all[:, j, :], p_kv[j % 4][:, D:2 * D]).then_inc(s_vc, 1)

            half = HD // 2
            W8 = TPB * G
            cos_b = cos_sb[:, :].unsqueeze(1).to_broadcast([P, UNITS, W8 * HD])
            sin_b = sin_sb[:, :].rearrange("p (w d) -> p w d", d=HD).unsqueeze(1).to_broadcast([P, UNITS, W8, HD])
            for qk in range(2):
                raw = qk_raw[:, qk, :]
                step(v.tensor_tensor(rope[:, :].rearrange("p (u w) -> p u w", u=UNITS),
                                     raw.rearrange("p (u w) -> p u w", u=UNITS), cos_b, ALU.mult))
                for o in range(2):
                    mine, other = slice(o * half, (o + 1) * half), slice((1 - o) * half, (2 - o) * half)
                    step(v.tensor_tensor(grouped(work[:, :])[:, :, :, mine], grouped(raw)[:, :, :, other],
                                         sin_b[:, :, :, mine], ALU.mult))
                v.tensor_tensor(rope[:, :], rope[:, :], work[:, :], ALU.add).then_inc(s_rope, 1)
                dve.wait_ge(s_part, 2 * qk + 1)
                v.tensor_tensor(grouped(rope[:, :]), grouped(rope[:, :]), product(qk, 0), ALU.subtract).then_inc(s_rope, 1)
                copies = ((1, 0), (2, 0)) if qk == 0 else ((3, 0), (5, 0))
                for to, of in copies:
                    step(v.tensor_copy(product(qk, to), product(qk, of)))
                dve.wait_ge(s_part, 2 * qk + 2)
                second, third = (3, 5) if qk == 0 else (1, 2)
                step(v.tensor_tensor(product(qk, third), grouped(rope[:, :]), product(qk, second), ALU.subtract))
                ins = v.tensor_copy(product(qk, 4), product(qk, second))
                if qk == 0:
                    step(ins)
                else:
                    ins.then_inc(s_stage, 1)

            dve.wait_ge(s_bias, 32)
            dve.wait_ge(s_expert, 1)

            def copy_xT(t, par):
                dve.wait_ge(xsT_done, t + 1)
                v.tensor_copy(xsT[par][:, :], p_xsT[:, 0:P]).then_inc(xsT_copied, 1)

            def add_bias(t, par, gelu_before):
                e = nc.vector.value_load(expert[0:1, bass.ds(t, 1)], min_val=0, max_val=E - 1)
                dve.wait_ge(pre_done, t + 1)
                if gelu_before:
                    dve.wait_ge(gelu_done, t - 1)
                v.tensor_tensor(pre[par], p_pre[par], b1_all[:, bass.ds(e * F, F)], ALU.add).then_inc(bias_done, 1)

            def finish_y(t, par, n_stored):
                e = nc.vector.value_load(expert[0:1, bass.ds(t, 1)], min_val=0, max_val=E - 1)
                dve.wait_ge(y_done, t + 1)
                if n_stored is not None:
                    dve.wait_ge(y_stored[par], n_stored)
                v.tensor_tensor(y_sb[par][:, :], p_y[:, 0:D], b2_all[:, bass.ds(e * D, D)], ALU.add).then_inc(y_copied, 1)

            for t in range(3):
                copy_xT(t, t % 2)
            add_bias(0, 0, False)
            add_bias(1, 1, False)
            for t in (0, 1):
                copy_xT(t + 3, 1 - t)
                add_bias(t + 2, t, True)
                finish_y(t, t, None)
            with dve.Fori(1, 10) as i:
                for par in range(2):
                    t = i * 2 + par
                    copy_xT(t + 3, 1 - par)
                    add_bias(t + 2, par, True)
                    finish_y(t, par, i * 16)
            for t in range(20, SLOT_TILES):
                if t + 3 < SLOT_TILES:
                    copy_xT(t + 3, 1 - t % 2)
                if t + 2 < SLOT_TILES:
                    add_bias(t + 2, t % 2, True)
                finish_y(t, t % 2, 16 * (t // 2))

            dve.wait_ge(s_lexp, 1)
            step(v.tensor_reduce(gsum[:, :], lexp[:, :].rearrange("p (j e) -> p j e", e=E), AX.X, ALU.add))
            v.reciprocal(gate[:, :], gsum[:, :]).then_inc(s_gate, 1)

            v.memset(recip, 0.0).then_inc(attn_zero, 1)
            v.memset(recip_last, 0.0).then_inc(attn_zero, 1)

            def read_scores(u, par):
                mv = mx[:, par, :].rearrange("p (t c a) -> p t c a", t=2, c=2)
                t0 = p_sm[0][:, :].rearrange("p (w n) -> p w n", n=P)
                t1 = p_sm[1][:, :].rearrange("p (a n) -> p a n", n=S)
                for k, (dst, src) in enumerate(((mv[:, 1, 0, :], t1), (mx[:, par, 0:4], t0), (mv[:, 1, 1, :], t1))):
                    dve.wait_ge(sm_done, u * 3 + k + 1)
                    v.tensor_reduce(dst, src, AX.X, ALU.max).then_inc(sm_read, 1)
                nv = nm[:, par, :].rearrange("p (t r w) -> p t r w", t=2, r=2)
                m2 = mx[:, par, :].rearrange("p (t w) -> p t w", t=2)
                dve.wait_ge(sm_read, u * 3 + 3)
                v.tensor_scalar(nv[:, :, 0, :], m2, -1.0, None, ALU.mult).then_inc(s_neg, 1)
                dve.wait_ge(s_neg, u + 1)
                v.scalar_tensor_tensor(nv[:, :, 1, :], m2, -1.0, nv[:, :, 0, :], ALU.mult, ALU.subtract).then_inc(nm_ready, 1)

            def copy_maxima(u, g):
                dve.wait_ge(nmT_done, u + 1)
                v.tensor_copy(nmT[g], p_mb[0:8, 0:S]).then_inc(nmT_copied, 1)

            def invert_sums(n):
                dve.wait_ge(den_landed, n * 32)
                v.reciprocal(inv, den).then_inc(inv_ready, 1)

            def normalise_half(i, n):
                dve.wait_ge(pv_done, n)
                q = slice(i * S, (i + 1) * S)
                v.reciprocal(recip_raw[:, q], p_o[:, q]).then_inc(s_rec, 1)
                dve.wait_ge(last_landed, 64 * (i + 1))
                v.tensor_tensor(attn_last[:, q], p_o[:, q], recip_last[:, q], ALU.mult).then_inc(half_ready, 1)

            def finish_rows(b, i=0, stored=None):
                dve.wait_ge(proj_done, b + 1)
                if stored is not None:
                    dve.wait_ge(s_out, stored)
                v.tensor_tensor(o_sb[i].rearrange("p (t d) -> p t d", t=TPB),
                                p_m[:, 0:TPB * D].rearrange("p (t d) -> p t d", t=TPB),
                                acc[:, bass.ds(b * TPB, TPB), :], ALU.add).then_inc(o_ready, 1)

            def attention_unit(s, g, b, maxima, scores, sums_too, rows_too):
                if rows_too and g == 2:
                    finish_rows(b - 2, stored=None if isinstance(b, int) and b == 2 else (b - 2) * 16)
                if maxima:
                    copy_maxima(s + 2, (g + 2) % GROUPS)
                if scores:
                    read_scores(s + 3, (g + 1) % 2)
                if sums_too and g == 2:
                    invert_sums(b)

            read_scores(0, 0)
            read_scores(1, 1)
            copy_maxima(0, 0)
            read_scores(2, 0)
            copy_maxima(1, 1)
            for g in range(GROUPS):
                attention_unit(g, g, 0, True, True, False, False)
            for g in range(GROUPS):
                attention_unit(GROUPS + g, g, 1, True, True, True, False)
            dve.wait_ge(s_acc, 2)
            for g in range(GROUPS):
                attention_unit(2 * GROUPS + g, g, 2, True, True, True, True)
            with dve.Fori(3, B - 1) as b:
                for g in range(GROUPS):
                    attention_unit(b * GROUPS + g, g, b, True, True, True, True)
            for g in range(GROUPS):
                attention_unit((B - 1) * GROUPS + g, g, B - 1, g < 2, g < 1, True, True)
            normalise_half(0, UNITS - 2)
            finish_rows(B - 2, stored=(B - 2) * 16)
            normalise_half(1, UNITS)
            finish_rows(B - 1, i=1)

        @block.tensor
        def _(pe):
            mm = nc.tensor.matmul
            tr = nc.tensor.transpose
            pe.wait_ge(s_const, 10)
            pe.wait_ge(s_xn, 1)
            for a in range(TILES // 4):
                if a >= 2:
                    pe.wait_ge(s_xnTc, a - 1)
                for k in range(4):
                    ins = tr(p_xnT[a % 2][:, k * P:(k + 1) * P], xn[:, 4 * a + k, :], ident[:, :])
                ins.then_inc(s_xnT, 1)
            pe.wait_ge(s_win, 48)
            for a in range(TILES // 2):
                pe.wait_ge(s_xnTc, a // 2 + 1)
                if a >= 2:
                    pe.wait_ge(s_qc, a - 1)
                    pe.wait_ge(s_lowc, a - 1)
                for t in range(2):
                    j = 2 * a + t
                    ins = mm(p_in[a % 2][:, t * 256:t * 256 + QP], xnT[:, j * P:(j + 1) * P], w_in[:, :], start=True, stop=True)
                ins.then_inc(s_in, 1)
            pe.wait_ge(s_onehot, 1)
            n = TILES * E
            mm(p_route[:, 0:n], before[:, :], onehot_b[:, :], start=True, stop=True)
            mm(p_route[:, n:2 * n], ones_b[:, :], onehot_b[:, :], start=True, stop=True).then_inc(s_rank, 1)
            pe.wait_ge(s_latn, 1)
            for a in range(4):
                ins = tr(p_latT[:, a * P:(a + 1) * P], latn[:, a * P:(a + 1) * P], ident[:, :])
            ins.then_inc(s_latT, 1)
            pe.wait_ge(s_latTc, 1)
            pe.wait_ge(s_small, 16 * 21)
            pe.wait_ge(s_qc, TILES // 2)
            for j in range(TILES):
                if j >= 4:
                    pe.wait_ge(s_vc, j - 3)
                r = slice(L * (j % 4), L * (j % 4 + 1))
                mm(p_kv[j % 4][:, 0:2 * D], latT[r, j // 4, :], w_kv[r, :], start=True, stop=True).then_inc(s_kv, 1)

            def rows_T(t, par, loaded, copied):
                pe.wait_ge(xs_loaded[par], loaded)
                if copied is not None:
                    pe.wait_ge(xsT_copied, copied)
                tr(p_xsT[:, 0:P], xs[par][:, :], ident[:, :]).then_inc(xsT_done, 1)

            def first_half(t, par, biased):
                e = nc.tensor.value_load(expert[0:1, bass.ds(t, 1)], min_val=0, max_val=E - 1)
                pe.wait_ge(xsT_copied, t + 1)
                if biased is not None:
                    pe.wait_ge(bias_done, biased)
                mm(p_pre[par], xsT[par][:, :], w1[:, bass.ds(e * F, F)], start=True, stop=True).then_inc(pre_done, 1)

            def hidden_T(t, par, copied):
                pe.wait_ge(gelu_done, t + 1)
                if copied is not None:
                    pe.wait_ge(hT_copied, copied)
                for c in range(FC):
                    ins = tr(p_hT[par][:, c * P:(c + 1) * P], hid[par][:, c * P:(c + 1) * P], ident[:, :])
                ins.then_inc(hT_done, 1)

            def second_half(t, par, copied):
                e = nc.tensor.value_load(expert[0:1, bass.ds(t, 1)], min_val=0, max_val=E - 1)
                pe.wait_ge(hT_copied, t + 1)
                if copied is not None:
                    pe.wait_ge(y_copied, copied)
                for c in range(FC):
                    ins = mm(p_y[:, 0:D], hidT[par][:, c * P:(c + 1) * P], w2[:, bass.ds(e * (FC * D) + c * D, D)],
                             start=(c == 0), stop=(c == FC - 1))
                ins.then_inc(y_done, 1)

            pe.wait_ge(s_expert, 1)
            pe.wait_ge(s_vc, TILES)
            rows_T(0, 0, 16, None)
            rows_T(1, 1, 16, 1)
            pe.wait_ge(s_w1, 16)
            first_half(0, 0, None)
            rows_T(2, 0, 32, 2)
            first_half(1, 1, None)
            pe.wait_ge(s_w2, 16)
            for t in (0, 1):
                hidden_T(t, t, None)
                rows_T(t + 3, 1 - t, 32 + 16 * t, t + 3)
                first_half(t + 2, t, t + 1)
                second_half(t, t, None if t == 0 else 1)
            with pe.Fori(1, 10) as i:
                for par in range(2):
                    t = i * 2 + par
                    hidden_T(t, par, t - 1)
                    rows_T(t + 3, 1 - par, i * 16 + 32 + 16 * par, t + 3)
                    first_half(t + 2, par, t + 1)
                    second_half(t, par, t)
            for t in range(20, SLOT_TILES):
                hidden_T(t, t % 2, t - 1)
                if t + 3 < SLOT_TILES:
                    rows_T(t + 3, (t + 3) % 2, 16 * ((t + 3) // 2 + 1), t + 3)
                if t + 2 < SLOT_TILES:
                    first_half(t + 2, t % 2, t + 1)
                second_half(t, t % 2, t)

            def stack(w, g, first=False):
                if not first:
                    pe.wait_ge(stk_copied, w)
                unit = stage[:, bass.ds(w * CH, CH)]
                for qk in range(2):
                    for a in range(2):
                        for t in range(TPB):
                            lo = ((qk * TPB + t) * G + 2 * a) * HW
                            to = (qk * 4 + a * 2 + t) * P
                            ins = tr(p_stk[:, to:to + P], unit[:, lo:lo + 2 * HW], ident_b[:, :])
                ins.then_inc(stk_done, 1)


            def mask(bk):
                mm(bk, ident_b[:, :], causal_neg[:, :].unsqueeze(1).to_broadcast([P, bk.shape[1], P]),
                   start=True, stop=False, skip_group_check=True)

            def by_query_tile0(g, c):
                for a in range(2):
                    to = (2 * c + a) * P
                    ins = mm(p_sm[0][:, to:to + P], q_rows(g, c, a, 0, P, ROWS), k_rows(g, c, a, 0, ROWS),
                             start=False, stop=(c == 1 and a == 1), skip_group_check=True)
                return ins

            def by_query_tile1(g, c):
                mask(p_sm[1][:, :].rearrange("p (a n) -> p a n", a=2)[:, :, P:S])
                for a in range(2):
                    ins = mm(p_sm[1][:, a * S:(a + 1) * S], q_rows(g, c, a, P, S, ROWS),
                             stk[g][64 * c:64 * c + ROWS, 1, a, 0:S], start=False, stop=(a == 1), skip_group_check=True)
                ins.then_inc(sm_done, 1)

            def scores_by_query(u, g, first=False):
                pe.wait_ge(stk_copied, u + 1)
                if not first:
                    pe.wait_ge(sm_read, u * 3)
                mask(p_sm[0][:, :].rearrange("p (w n) -> p w n", w=G))
                by_query_tile0(g, 0).then_inc(sm_half, 1)
                by_query_tile1(g, 0)
                pe.wait_ge(sm_half, u + 1)
                by_query_tile0(g, 1).then_inc(sm_done, 1)

            def scores_by_query_rest(u, g):
                pe.wait_ge(sm_read, u * 3 + 1)
                by_query_tile1(g, 1)

            def scores_by_key(s, g, landed, first=False):
                pe.wait_ge(m_landed[g], landed)
                if not first:
                    pe.wait_ge(exp_done, s)
                for c in range(2):
                    for a in range(2):
                        to = (2 * c + a) * S
                        mm(p_st[:, to:to + S], k_rows(g, c, a, 0, SH), q_rows(g, c, a, 0, S, SH), start=True, stop=True)
                    if c == 1:
                        pe.wait_ge(st_half, s + 1)
                    for a in range(2):
                        to = G * S + (2 * c + a) * P
                        ins = mm(p_st[:, to:to + P], k_rows(g, c, a, 1, SH), q_rows(g, c, a, P, S, SH), start=True, stop=True)
                    ins.then_inc(st_done if c else st_half, 1)

            def weigh_values(s, g):
                pe.wait_ge(mask_done, s * 2 + 2)
                pe.wait_ge(v_placed, s + 1)
                q = S * (g // 2)
                for t in range(TPB):
                    lo, n = (0, S) if t == 0 else (G * S, P)
                    for a in range(2):
                        for c in range(2):
                            r, h, k = 64 * (g % 2) + 32 * c, 2 * a + c, 2 * c + a
                            ins = mm(p_o[r:r + 32, q + S - n:q + S], v_pad[g][:, (t * G + h) * VW:(t * G + h + 1) * VW],
                                     probs[g % 2][:, lo + k * n:lo + (k + 1) * n],
                                     start=(t == 0 and a == 0), stop=(t == 1 and a == 1))
                ins.then_inc(pv_done, 1)

            def maxima_T(u, par):
                pe.wait_ge(nm_ready, u + 1)
                for t in range(TPB):
                    ins = tr(p_mb[0:8, t * P:(t + 1) * P], nm[:, par, 8 * t:8 * t + 8], ident_b[:, :])
                ins.then_inc(nmT_done, 1)

            def project(rows):
                for t in range(TPB):
                    for i in range(2):
                        ins = mm(p_m[:, t * D:(t + 1) * D], rows[:, i * S + t * P:i * S + (t + 1) * P], w_o[:, i, :],
                                 start=(i == 0), stop=(i == 1))
                ins.then_inc(proj_done, 1)

            def attention_unit(s, g, b, more_stack, more_scores, more_maxima, sums_too, rows_too):
                scores_by_key(s, g, (b + 1) * 32, first=not sums_too and g == 0)
                if more_maxima:
                    if g == 2 and rows_too:
                        pe.wait_ge(o_ready, b - 1)
                    else:
                        pe.wait_ge(nmT_copied, s + 2)
                    maxima_T(s + 2, g % 2)
                if more_scores:
                    scores_by_query(s + 3, (g + 3) % GROUPS)
                if more_stack:
                    stack(s + 4, g)
                if more_scores:
                    scores_by_query_rest(s + 3, (g + 3) % GROUPS)
                if rows_too and g == 1:
                    pe.wait_ge(nmT_copied, s + 3)
                    pe.wait_ge(attn_ready, b - 1)
                    project(attn)
                if sums_too or g > 0:
                    if g == 1 and sums_too:
                        pe.wait_ge(sums_copied, b)
                    if g == 3 and not more_stack:
                        pe.wait_ge(half_ready, 1)
                    weigh_values(s - 1, (g + 3) % GROUPS)

            pe.wait_ge(y_copied, SLOT_TILES)
            pe.wait_ge(s_stage, 1)
            stack(0, 0, first=True)
            stack(1, 1)
            scores_by_query(0, 0, first=True)
            scores_by_query_rest(0, 0)
            stack(2, 2)
            scores_by_query(1, 1)
            scores_by_query_rest(1, 1)
            maxima_T(0, 0)
            stack(3, 3)
            scores_by_query(2, 2)
            scores_by_query_rest(2, 2)
            pe.wait_ge(nmT_copied, 1)
            maxima_T(1, 1)
            for g in range(GROUPS):
                attention_unit(g, g, 0, True, True, True, False, False)
            for g in range(GROUPS):
                attention_unit(GROUPS + g, g, 1, True, True, True, True, False)
            with pe.Fori(2, B - 1) as b:
                for g in range(GROUPS):
                    attention_unit(b * GROUPS + g, g, b, True, True, True, True, True)
            for g in range(GROUPS):
                attention_unit((B - 1) * GROUPS + g, g, B - 1, False, g == 0, g < 2, True, True)
            weigh_values(UNITS - 1, GROUPS - 1)
            pe.wait_ge(o_ready, B - 2)
            pe.wait_ge(attn_ready, B - 1)
            project(attn)
            pe.wait_ge(o_ready, B - 1)
            pe.wait_ge(half_ready, 2)
            project(attn_last)


_IN = ["x", "W_q", "W_dkv", "W_uk", "W_uv", "W_o", "ln_gamma", "ln_beta", "W1", "b1", "W2", "b2", "Wr", "br", "cos", "sin"]


def kernel(L0_attn_x, L0_attn_W_q, L0_attn_W_dkv, L0_attn_W_uk, L0_attn_W_uv, L0_attn_W_o, L0_attn_ln_gamma,
           L0_attn_ln_beta, L0_ffn_W1, L0_ffn_b1, L0_ffn_W2, L0_ffn_b2, L0_ffn_Wr, L0_ffn_br):
    import numpy as np
    import concourse.bacc as bacc
    from concourse.bass_utils import run_bass_kernel_spmd

    half = HD // 2
    inv_freq = (np.float32(1.0) / np.power(np.float32(10000.0), np.arange(half, dtype=np.float32) / np.float32(half))).astype(np.float32)
    angle = (np.arange(S, dtype=np.float32)[:, None] * inv_freq[None, :]).astype(np.float32)
    cos = np.concatenate([np.cos(angle)] * 2, axis=1).astype(np.float32)
    sin = np.concatenate([-np.sin(angle), np.sin(angle)], axis=1).astype(np.float32)

    def table(t):
        t = t.reshape(TPB, P, 1, HD).transpose(1, 0, 2, 3)
        return np.ascontiguousarray(np.broadcast_to(t, (P, TPB, G, HD)).reshape(P, TPB * G * HD))

    values = [L0_attn_x, L0_attn_W_q, L0_attn_W_dkv, L0_attn_W_uk, L0_attn_W_uv, L0_attn_W_o, L0_attn_ln_gamma,
              L0_attn_ln_beta, L0_ffn_W1, L0_ffn_b1, L0_ffn_W2, L0_ffn_b2, L0_ffn_Wr, L0_ffn_br, table(cos), table(sin)]
    nc = bacc.Bacc("TRN2", target_bir_lowering=False, num_devices=1)
    arrays, args = {}, []
    for name, value in zip(_IN, values):
        a = np.ascontiguousarray(value)
        arrays[f"in_{name}"] = a
        args.append(nc.dram_tensor(f"in_{name}", a.shape, mybir.dt.from_np(a.dtype), kind="ExternalInput").ap())
    out = nc.dram_tensor("out_rows", (B, S, D), F32, kind="ExternalOutput").ap()
    layer_program(nc, *args, out)
    r = run_bass_kernel_spmd(nc, [arrays], core_ids=[0])
    return r.results[0]["out_rows"]
```

```python
from contextlib import ExitStack

import concourse.bass as bass
from concourse import mybir

F32 = mybir.dt.float32
BF16 = mybir.dt.bfloat16
I32 = mybir.dt.int32
ALU = mybir.AluOpType
ACT = mybir.ActivationFunctionType
AX = mybir.AxisListType

P = 128
B, S, D = 8, 256, 128
H, HD = 16, 8
L = 32
E, F = 8, 512
EPS = 1e-5
TILES = B * S // P
TPB = S // P
FC = F // P
SLOT_TILES = TILES + E - 1
G = 4
GROUPS = H // G
UNITS = B * GROUPS
Q_PARTS = (1, 1, 2, 1, 3, 2)
K_PARTS = (1, 2, 1, 3, 1, 2)
PARTS = len(Q_PARTS)
ROWS = PARTS * HD
SH = ROWS + 2
QP = D + L + E
HW = 64
CH = 2 * TPB * G * HW
VW = 32
STW = G * (S + P)
NEG = -1.0e30


def layer_program(nc, x, W_q, W_dkv, W_uk, W_uv, W_o, ln_gamma, ln_beta, W1, b1, W2, b2, Wr, br, cos_t, sin_t, out):
    ctx = ExitStack()
    with ctx:
        def sb(name, shape, dt=F32):
            return ctx.enter_context(nc.sbuf_tensor(name, shape, dt))

        def sem(name):
            return ctx.enter_context(nc.semaphore(name))

        x_sb = sb("x_sb", [P, TILES, D])
        w_in = sb("w_in", [P, QP])
        w_kv = sb("w_kv", [P, 2 * D])
        w_o = sb("w_o", [P, 2, D])
        w1 = sb("w1", [P, E * F])
        w2 = sb("w2", [P, E * FC * D])
        b1_all = sb("b1_all", [P, E * F])
        b2_all = sb("b2_all", [P, E * D])
        gamma = sb("gamma", [P, L])
        beta = sb("beta", [P, L])
        br_all = sb("br_all", [P, E])
        cos_sb = sb("cos_sb", [P, TPB * G * HD])
        sin_sb = sb("sin_sb", [P, TPB * G * HD])
        ident = sb("ident", [P, P])
        ident_b = sb("ident_b", [P, P], BF16)
        before = sb("before", [P, P], BF16)
        ones_b = sb("ones_b", [P, P], BF16)
        den_rows = sb("den_rows", [P, P])
        causal_neg = sb("causal_neg", [P, P], BF16)
        tick = sb("tick", [P, 2])
        zeros = sb("zeros", [P, 4 * D])
        rank_of_e = sb("rank_of_e", [P, E])
        mult128 = sb("mult128", [P, TILES])
        tile_no = sb("tile_no", [P, SLOT_TILES])

        xn = sb("xn", [P, TILES, D])
        xnT = sb("xnT", [P, TILES * P])
        work = sb("work", [P, TILES * D])
        rope = sb("rope", [P, TILES * D])
        qk_raw = sb("qk_raw", [P, 2 * TILES * D])
        swapped = rope[:, 0:2 * S]
        same = rope[:, 2 * S:4 * S]
        low = sb("low", [P, TILES, L + E])
        latn = sb("latn", [P, TILES * L])
        latT = sb("latT", [P, 4, P])
        st = sb("st", [P, 12, TILES])
        bn = sb("bn", [P, TILES, 6])
        mean_var = sb("mean_var", [P, TILES, 2])
        shift = sb("shift", [P, TILES])
        rt = sb("rt", [P, 12, TILES * E])
        onehot_b = sb("onehot_b", [P, (TILES + 1) * E], BF16)
        nte = sb("nte", [P, 6, E])
        lower = sb("lower", [P, E, E])
        cmp = sb("cmp", [P, SLOT_TILES * E])
        slot_f = sb("slot_f", [P, TILES])
        slot = sb("slot", [P, TILES], I32)
        expert_f = sb("expert_f", [P, SLOT_TILES])
        expert = sb("expert", [P, SLOT_TILES], I32)
        gate = sb("gate", [P, TILES])
        gsum = sb("gsum", [P, TILES])
        lshift = sb("lshift", [P, TILES * E])
        lexp = sb("lexp", [P, TILES * E])

        xs = [sb(f"xs{i}", [P, D]) for i in range(2)]
        xsT = [sb(f"xsT{i}", [P, P]) for i in range(2)]
        pre = [xnT[:, i * F:(i + 1) * F] for i in range(2)]
        hid = [xnT[:, (2 + i) * F:(3 + i) * F] for i in range(2)]
        hidT = [rope[:, 4 * S + i * F:4 * S + (i + 1) * F] for i in range(2)]
        y_sb = [sb(f"y_sb{i}", [P, D]) for i in range(2)]
        acc = xn

        stage = sb("stage", [P, UNITS * CH], BF16)
        stk = [work[:, g * 2 * S:(g + 1) * 2 * S].bitcast(BF16).rearrange("p (k a t) -> p k a t", k=2, a=2)
               for g in range(GROUPS)]
        def stk_flat(g):
            return work[:, g * 2 * S:(g + 1) * 2 * S].bitcast(BF16)

        mx = sb("mx", [P, 2, 8])
        nm = sb("nm", [P, 2, 16], BF16)
        nmT = [latn[0:8, g * S // 2:(g + 1) * S // 2].bitcast(BF16) for g in range(GROUPS)]
        probs = [qk_raw[:, i * TILES * D:i * TILES * D + STW] for i in range(2)]
        v_all = sb("v_all", [P, TILES, D])
        VP = TPB * G * VW
        v_pad = [b1_all[:, g * VP:(g + 1) * VP] for g in range(GROUPS)]
        attn = rope[:, 0:2 * S]
        recip = rope[:, 2 * S:4 * S]
        o_sb = [rope[:, 6 * S + i * TPB * D:6 * S + (i + 1) * TPB * D] for i in range(2)]
        sums_of = w1
        attn_last = qk_raw[:, TILES * D + STW:]
        l3 = latn[:, :].rearrange("p (j l) -> p j l", l=L)
        lat_g = rope[:, 0:TILES * L].rearrange("p (j l) -> p j l", l=L)
        lat_sq = work[:, 0:TILES * L].rearrange("p (j l) -> p j l", l=L)
        spare = low[:, :, :].rearrange("p j w -> p (j w)")
        recip_last = spare[:, 0:2 * S]
        SEG = 2 * S // (P // 8)
        den = spare[:, 2 * S:2 * S + SEG]
        inv = spare[:, 2 * S + SEG:2 * S + 2 * SEG]

        xs_dram = nc.dram_tensor("xs_dram", [SLOT_TILES * P, D], F32, kind="Internal").ap()
        inv_dram = nc.dram_tensor("inv_dram", [8, 2 * S], F32, kind="Internal").ap()
        ys_dram = nc.dram_tensor("ys_dram", [SLOT_TILES * P, D], F32, kind="Internal").ap()

        wide = ctx.enter_context(nc.psum_tensor("wide", [P, 3 * 512], F32))
        bank = [ctx.enter_context(nc.psum_tensor(f"bank{i}", [P, 512], F32)) for i in range(5)]
        p_xnT = [wide[:, 0:512], wide[:, 512:1024]]
        p_in = [bank[0], bank[1], bank[3], bank[4]]
        p_route = bank[2]
        p_latT = wide[:, 1024:1536]
        p_kv = [bank[3], bank[4], bank[0], bank[1]]
        p_pre = [wide[:, 0:512], wide[:, 512:1024]]
        p_hT = [wide[:, 1024:1536], bank[0][:, :]]
        p_xsT = bank[1]
        p_y = bank[2]
        p_st = wide
        p_sm = [bank[0][:, :], bank[1][:, :]]
        p_sm_early = [bank[1][:, :], wide[:, 512:1024]]
        p_o = bank[2]
        p_stk = bank[3][:, :].bitcast(BF16)
        p_den = [bank[3][:, 0:S], bank[0][:, 0:S]]
        p_m = bank[4]
        p_last = bank[1]
        p_mb = bank[4][:, :].bitcast(BF16)

        s_x = [sem(f"s_x{i}") for i in range(4)]
        s_win = sem("s_win")
        s_small = sem("s_small")
        s_w1 = sem("s_w1")
        s_w2 = sem("s_w2")
        s_bias = sem("s_bias")
        s_zero = sem("s_zero")
        s_init = sem("s_init")
        s_const = sem("s_const")
        s_pad = sem("s_pad")
        s_rows = sem("s_rows")
        s_dve = sem("s_dve")
        s_bn = sem("s_bn")
        s_mean = sem("s_mean")
        s_shift = sem("s_shift")
        s_latsum = sem("s_latsum")
        s_latsub = sem("s_latsub")
        s_latg = sem("s_latg")
        s_latsq = sem("s_latsq")
        s_var = sem("s_var")
        s_root = sem("s_root")
        s_xn = sem("s_xn")
        s_xna = sem("s_xna")
        s_xnT = sem("s_xnT")
        s_xnTc = sem("s_xnTc")
        s_in = sem("s_in")
        s_qc = sem("s_qc")
        s_lowc = sem("s_lowc")
        s_onehot = sem("s_onehot")
        s_rank = sem("s_rank")
        s_slot = sem("s_slot")
        s_expert = sem("s_expert")
        s_latvar = sem("s_latvar")
        s_latroot = sem("s_latroot")
        s_latn = sem("s_latn")
        s_latT = sem("s_latT")
        s_latTc = sem("s_latTc")
        s_kv = sem("s_kv")
        s_kc = sem("s_kc")
        s_vc = sem("s_vc")
        s_rope = sem("s_rope")
        s_tick = sem("s_tick")
        s_rotated = sem("s_rotated")
        s_part1 = sem("s_part1")
        s_left = sem("s_left")
        s_part2 = sem("s_part2")
        s_stage = sem("s_stage")
        s_scat = sem("s_scat")
        xs_loaded = [sem(f"xs_loaded{i}") for i in range(2)]
        xsT_done = sem("xsT_done")
        xsT_copied = sem("xsT_copied")
        pre_done = sem("pre_done")
        bias_done = sem("bias_done")
        gelu_done = sem("gelu_done")
        hT_done = sem("hT_done")
        hT_copied = sem("hT_copied")
        y_done = sem("y_done")
        y_copied = sem("y_copied")
        y_stored = [sem(f"y_stored{i}") for i in range(2)]
        s_gath = sem("s_gath")
        s_lexp = sem("s_lexp")
        s_gate = sem("s_gate")
        s_scaled = sem("s_scaled")
        s_acc = sem("s_acc")
        stk_done = sem("stk_done")
        stk_copied = sem("stk_copied")
        sm_done = sem("sm_done")
        sm_read = sem("sm_read")
        sm_half = sem("sm_half")
        st_half = sem("st_half")
        nm_ready = sem("nm_ready")
        nmT_done = sem("nmT_done")
        nmT_copied = sem("nmT_copied")
        m_landed = [sem(f"m_landed{g}") for g in range(GROUPS)]
        st_done = sem("st_done")
        exp_done = sem("exp_done")
        mask_done = sem("mask_done")
        pv_done = sem("pv_done")
        attn_ready = sem("attn_ready")
        v_placed = sem("v_placed")
        proj_done = sem("proj_done")
        o_ready = sem("o_ready")
        s_neg = sem("s_neg")
        s_rec = sem("s_rec")
        sums_copied = sem("sums_copied")
        den_landed = sem("den_landed")
        inv_ready = sem("inv_ready")
        inv_stored = sem("inv_stored")
        inv_landed = sem("inv_landed")
        attn_zero = sem("attn_zero")
        half_ready = sem("half_ready")
        half_copied = sem("half_copied")
        den_done = sem("den_done")
        s_out = sem("s_out")

        x_rows = x.rearrange("b t d -> (b t) d").rearrange("(j p) d -> p j d", p=P)
        out_rows = out.rearrange("b t d -> (b t) d").rearrange("(j p) d -> p j d", p=P)

        def mul(a, k):
            return a if k == 1 else a * k

        def rows_of(b):
            return qk_raw[:, bass.ds(b * 2 * S, 2 * S)].rearrange("p (g w d) -> p g w d", g=GROUPS, d=HD)

        def staged(b, n):
            return stage[:, bass.ds(b * GROUPS * CH, GROUPS * CH)].rearrange(
                "p (g w c) -> p g w c", g=GROUPS, c=HW)[:, :, :, n * HD:(n + 1) * HD]

        def of(qk, ap):
            return ap[:, :, qk * TPB * G:(qk + 1) * TPB * G, :]

        def k_rows(g, c, a, tile, rows):
            return stk[g][64 * c:64 * c + rows, 1, a, tile * P:(tile + 1) * P]

        def q_rows(g, c, a, lo, hi, rows):
            return stk[g][64 * c:64 * c + rows, 0, a, lo:hi]

        def pad_columns(g, shift):
            ap = [[E * F, P], [G * VW, TPB], [2 * VW + HD, 2], [VW, 2], [1, HD]]
            return bass.AP(tensor=b1_all, offset=g * VP + shift, ap=ap)

        def load_x(engine, i):
            j = slice(i * TILES // 4, (i + 1) * TILES // 4)
            engine.dma_start(x_sb[:, j, :], x_rows[:, j, :]).then_inc(s_x[i], 16)

        block = ctx.enter_context(nc.Block())

        @block.sync
        def _(sp):
            load_x(sp, 0)
            load_x(sp, 2)
            sp.dma_start(w_in[:, 0:D], W_q).then_inc(s_win, 16)
            sp.dma_start(w_in[:, D:D + L], W_dkv).then_inc(s_win, 16)
            sp.dma_start(w_in[:, D + L:QP], Wr).then_inc(s_win, 16)
            for i in range(4):
                sp.dma_start(w_kv[L * i:L * (i + 1), 0:D], W_uk).then_inc(s_small, 16)
                sp.dma_start(w_kv[L * i:L * (i + 1), D:2 * D], W_uv).then_inc(s_small, 16)
            sp.dma_start(gamma[:, :], ln_gamma.partition_broadcast(P)).then_inc(s_small, 16)
            sp.dma_start(beta[:, :], ln_beta.partition_broadcast(P)).then_inc(s_small, 16)
            sp.dma_start(br_all[:, :], br.partition_broadcast(P)).then_inc(s_small, 16)
            sp.dma_start(cos_sb[:, :], cos_t).then_inc(s_small, 16)
            sp.dma_start(sin_sb[:, :], sin_t).then_inc(s_small, 16)
            sp.wait_ge(s_init, 11)
            for g in range(GROUPS):
                for c in range(2):
                    r = 64 * (g % 2) + 32 * c
                    src = W_o.rearrange("(g a c d) n -> g c a d n", g=GROUPS, a=2, c=2)[g, c]
                    sp.dma_start(w_o[r:r + 2 * HD, g // 2, :], src).then_inc(s_small, 16)
            sl = xs_dram.rearrange("(n p) d -> p n d", p=P)
            for n in range(0, SLOT_TILES, 4):
                k = min(4, SLOT_TILES - n)
                sp.dma_start(sl[:, n:n + k, :], zeros[:, 0:k * D].rearrange("p (k d) -> p k d", d=D)).then_inc(s_zero, 16)
            sp.dma_start(w1[:, :].rearrange("p (e f) -> p e f", e=E), W1.rearrange("e d f -> d e f")).then_inc(s_w1, 16)
            sp.dma_start(w2[:, :].rearrange("p (e c n) -> p e c n", e=E, c=FC),
                         W2.rearrange("e (c p) n -> p e c n", p=P)).then_inc(s_w2, 16)
            sp.dma_start(b1_all[:, :], b1.rearrange("e f -> (e f)").partition_broadcast(P)).then_inc(s_bias, 16)
            sp.dma_start(b2_all[:, :], b2.rearrange("e f -> (e f)").partition_broadcast(P)).then_inc(s_bias, 16)

            def load_slots(t, par):
                sp.dma_start(xs[par][:, :], xs_dram[bass.ds(t * P, P), :]).then_inc(xs_loaded[par], 16)

            def store_y(t, par):
                sp.wait_ge(y_copied, t + 1)
                sp.dma_start(ys_dram[bass.ds(t * P, P), :], y_sb[par][:, :]).then_inc(y_stored[par], 16)

            sp.wait_ge(s_scat, 16 * TILES)
            load_slots(0, 0)
            load_slots(1, 1)
            for t in (2, 3, 4):
                sp.wait_ge(xsT_done, t - 1)
                load_slots(t, t % 2)

            def expert_slot(t, par, load):
                if load:
                    sp.wait_ge(xsT_done, t + 4)
                    load_slots(t + 5, 1 - par)
                store_y(t, par)

            for t in (0, 1):
                expert_slot(t, t, True)
            with sp.Fori(2, 16, 2) as t:
                for par in range(2):
                    expert_slot(t + par, par, True)
            def place_maxima(u, g):
                sp.wait_ge(nmT_copied, u + 1)
                for part in range(2):
                    sp.dma_start(stk[g][ROWS + part:P:64, 0, :, :], nmT[g][4 * part:4 * part + 4, :]).then_inc(m_landed[g], 16)

            for t in range(16, SLOT_TILES):
                if t == SLOT_TILES - 1:
                    place_maxima(0, 0)
                expert_slot(t, t % 2, t + 5 < SLOT_TILES)

            place_maxima(1, 1)

            def spread_sums(n):
                sp.wait_ge(sums_copied, n)
                sums = sums_of[:, bass.ds((n - 1) * 2 * S, 2 * S)]
                for i in range(2):
                    sp.dma_start(den[64 * i:64 * (i + 1), :], sums[(2 + i) * HD:P:32, :]).then_inc(den_landed, 16)

            def store_inverses(n):
                sp.wait_ge(inv_ready, n)
                sp.dma_start(inv_dram.rearrange("r (s k) -> (r s) k", k=SEG), inv).then_inc(inv_stored, 16)

            def load_inverses(n):
                sp.wait_ge(inv_stored, n * 16)
                if not isinstance(n, int) or n > 1:
                    sp.wait_ge(attn_ready, n - 1)
                for j in range(4):
                    src = inv_dram.rearrange("(a j) q -> j a q", j=4)[j].unsqueeze(1).to_broadcast([2, HD, 2 * S])
                    sp.dma_start(recip[32 * j:32 * j + 2 * HD, :], src).then_inc(inv_landed, 16)

            def store_rows(b):
                sp.wait_ge(o_ready, b + 1)
                sp.dma_start(out_rows[:, bass.ds(b * TPB, TPB), :],
                             o_sb[0].rearrange("p (t d) -> p t d", t=TPB)).then_inc(s_out, 16)

            def attention_unit(s, g, b, maxima, sums_too, rows_too):
                if sums_too and g == 1:
                    spread_sums(b)
                if maxima:
                    place_maxima(s + 2, (g + 2) % GROUPS)
                if sums_too and g == 2:
                    store_inverses(b)
                if sums_too and g == 3:
                    load_inverses(b)
                if rows_too and g == 3:
                    store_rows(b - 2)

            sp.wait_ge(attn_zero, 1)
            for b in range(2):
                for g in range(GROUPS):
                    attention_unit(b * GROUPS + g, g, b, True, b > 0, b > 1)
            with sp.Fori(2, B - 1) as b:
                for g in range(GROUPS):
                    attention_unit(b * GROUPS + g, g, b, True, True, True)
            for g in range(GROUPS):
                attention_unit((B - 1) * GROUPS + g, g, B - 1, g < 2, True, True)
            store_rows(B - 2)
            sp.wait_ge(o_ready, B)
            sp.dma_start(out_rows[:, (B - 1) * TPB:, :],
                         o_sb[1].rearrange("p (t d) -> p t d", t=TPB)).then_inc(s_out, 16)
            sp.wait_ge(s_out, 16 * B)

        @block.gpsimd
        def _(pool):
            pool.memset(ident[:, :], 0.0).then_inc(s_init, 1)
            pool.memset(ident_b[:, :], 0.0).then_inc(s_init, 1)
            pool.memset(ones_b[:, :], 1.0).then_inc(s_init, 1)
            pool.memset(den_rows[:, :], 0.0).then_inc(s_init, 1)
            pool.memset(before[:, :], 1.0).then_inc(s_init, 1)
            pool.memset(causal_neg[:, :], 0.0).then_inc(s_init, 1)
            pool.memset(zeros[:, :], 0.0).then_inc(s_init, 1)
            pool.memset(tick[:, :], 0.0).then_inc(s_init, 1)
            pool.memset(lower[:, :, :], 1.0).then_inc(s_init, 1)
            pool.memset(onehot_b[:, TILES * E:], 0.0).then_inc(s_init, 1)
            pool.memset(w_o[:, :, :], 0.0).then_inc(s_init, 1)
            pool.wait_ge(s_init, 11)
            for m in (ident, ident_b):
                pool.affine_select(out=m[:, :], in_=m[:, :], compare_op=ALU.not_equal, fill=1.0, base=0,
                                   pattern=[[-1, P]], channel_multiplier=1).then_inc(s_const, 1)
            pool.affine_select(out=den_rows[:, :], in_=den_rows[:, :], compare_op=ALU.not_equal, fill=1.0, base=-2 * HD,
                               pattern=[[-4 * HD, 4], [0, 2], [-1, 2 * HD]], channel_multiplier=1).then_inc(s_const, 1)
            pool.affine_select(out=lower[:, :, :], in_=lower[:, :, :], compare_op=ALU.is_gt, fill=0.0, base=0,
                               pattern=[[1, E], [-1, E]], channel_multiplier=0).then_inc(s_const, 1)
            pool.affine_select(out=before[:, :], in_=before[:, :], compare_op=ALU.is_gt, fill=0.0, base=0,
                               pattern=[[1, P]], channel_multiplier=-1).then_inc(s_const, 1)
            pool.affine_select(out=causal_neg[:, :], in_=causal_neg[:, :], compare_op=ALU.is_ge, fill=NEG,
                               base=0, pattern=[[-1, P]], channel_multiplier=1).then_inc(s_const, 1)
            pool.iota(rank_of_e[:, :], pattern=[[-1, E]], base=E, channel_multiplier=0,
                      allow_small_or_imprecise_dtypes=True).then_inc(s_const, 1)
            pool.iota(mult128[:, :], pattern=[[P, TILES]], base=0, channel_multiplier=0,
                      allow_small_or_imprecise_dtypes=True).then_inc(s_const, 1)
            pool.iota(tile_no[:, :], pattern=[[1, SLOT_TILES]], base=0, channel_multiplier=0,
                      allow_small_or_imprecise_dtypes=True).then_inc(s_const, 1)
            mrows = stage[:, :].rearrange("p (u k w c) -> p k u w c", u=UNITS, k=2, c=HW)
            for qk, lo, hi, value in ((0, ROWS, HW, 0.0), (1, ROWS, SH, 1.0), (1, SH, HW, 0.0)):
                pool.memset(mrows[:, qk, :, :, lo:hi], value).then_inc(s_rows, 1)

            def per_tile(ap):
                return ap.unsqueeze(2).to_broadcast([P, TILES, L])

            pool.wait_ge(s_latsum, 1)
            pool.tensor_tensor(l3, low[:, :, 0:L], per_tile(st[:, 0, :]), ALU.subtract).then_inc(s_latsub, 1)
            pool.wait_ge(s_latsub, 1)
            pool.wait_ge(s_small, 16 * 21)
            pool.tensor_tensor(lat_g, l3, gamma[:, :].unsqueeze(1).to_broadcast([P, TILES, L]), ALU.mult).then_inc(s_latg, 1)
            pool.wait_ge(s_slot, 1)
            pool.wait_ge(s_xn, TILES - TILES // 4)
            pool.wait_ge(s_xna, TILES // 4)
            pool.wait_ge(s_zero, 16 * ((SLOT_TILES + 3) // 4))
            for j in range(TILES):
                pool.indirect_dma_start(out=xs_dram, out_offset=bass.IndirectOffsetOnAxis(slot[:, j:j + 1], 0),
                                        in_=xn[:, j, :], in_offset=None).then_inc(s_scat, 16)

            def rotate(b, first=False):
                cos_b = cos_sb[:, :].unsqueeze(1).to_broadcast([P, 2 * GROUPS, TPB * G * HD])
                sin_b = sin_sb[:, :].rearrange("p (w d) -> p w d", d=HD).unsqueeze(1).to_broadcast([P, 2 * GROUPS, TPB * G, HD])
                raw = qk_raw[:, bass.ds(b * 2 * S, 2 * S)]
                raw4, other4 = [ap.rearrange("p (u w d) -> p u w d", u=2 * GROUPS, d=HD) for ap in (raw, swapped)]
                half = HD // 2
                if not first:
                    pool.wait_ge(s_rotated, b)
                    pool.wait_ge(s_tick, b * 2)
                    pool.tensor_tensor(tick[:, 1:2], tick[:, 0:1], tick[:, 0:1], ALU.add).then_inc(s_tick, 1)
                for o in range(2):
                    mine, other = slice(o * half, (o + 1) * half), slice((1 - o) * half, (2 - o) * half)
                    pool.tensor_tensor(other4[:, :, :, mine], raw4[:, :, :, other], sin_b[:, :, :, mine], ALU.mult).then_inc(s_rope, 1)
                raw3, same3 = [ap.rearrange("p (u w) -> p u w", u=2 * GROUPS) for ap in (raw, same)]
                pool.tensor_tensor(same3, raw3, cos_b, ALU.mult).then_inc(s_rope, 1)
                pool.wait_ge(s_rope, b * 3 + 3)
                if not first:
                    pool.wait_ge(s_tick, b * 2 + 1)
                pool.tensor_tensor(tick[:, 1:2], tick[:, 0:1], tick[:, 0:1], ALU.add).then_inc(s_tick, 1 + first)
                pool.tensor_tensor(raw, same, swapped, ALU.add).then_inc(s_rotated, 1)

            pool.wait_ge(s_small, 16 * 21)
            pool.wait_ge(s_qc, TILES // 2)
            pool.wait_ge(s_kc, TILES)
            rotate(0, first=True)
            with pool.Fori(1, B) as b:
                rotate(b)

            pool.wait_ge(bias_done, SLOT_TILES)
            pool.memset(b1_all[:, 0:GROUPS * VP], 0.0).then_inc(s_pad, 1)
            pool.wait_ge(s_pad, 1)
            for g in range(GROUPS):
                pool.memset(pad_columns(g, 2 * HD), 1.0).then_inc(s_pad, 1)

            def gather_results(j):
                pool.indirect_dma_start(out=acc[:, j, :], out_offset=None, in_=ys_dram,
                                        in_offset=bass.IndirectOffsetOnAxis(slot[:, j:j + 1], 0)).then_inc(s_gath, 16)

            def mask_unit(s, par, first=False, normalised=None, added=None):
                pool.wait_ge(exp_done, s + 1)
                if not first:
                    pool.wait_ge(mask_done, s * 2)
                if normalised is not None:
                    pool.wait_ge(attn_ready, normalised)
                if added is not None:
                    pool.wait_ge(s_acc, added)
                pool.tensor_tensor(tick[:, 1:2], tick[:, 0:1], tick[:, 0:1], ALU.add)
                early = probs[par][:, 0:G * S].rearrange("p (h q) -> p h q", h=G)[:, :, 0:P]
                late = probs[par][:, G * S:STW].rearrange("p (h q) -> p h q", h=G)
                for part in (early, late):
                    pool.affine_select(out=part, in_=part, compare_op=ALU.is_ge, fill=0.0, base=0,
                                       pattern=[[0, G], [1, P]], channel_multiplier=-1).then_inc(mask_done, 1)

            def place_values(u, g, b, first=False):
                if not first:
                    pool.wait_ge(pv_done, u - 3)
                src = v_all[:, bass.ds(b * TPB, TPB), g * G * HD:(g + 1) * G * HD].rearrange(
                    "p t (h d) -> p t h d", h=G)
                pool.tensor_copy(pad_columns(g, 0), src).then_inc(v_placed, 1)

            pool.wait_ge(s_vc, TILES)
            pool.wait_ge(s_pad, 1 + GROUPS)
            for u in range(2):
                place_values(u, u, 0, first=True)
            pool.wait_ge(s_tick, B * 2)
            for s in range(GROUPS):
                mask_unit(s, s % 2, first=(s == 0))
                place_values(s + 2, (s + 2) % GROUPS, (s + 2) // GROUPS, first=(s < 2))
                if s == 0:
                    pool.wait_ge(y_stored[0], 16 * ((SLOT_TILES + 1) // 2))
                    pool.wait_ge(y_stored[1], 16 * (SLOT_TILES // 2))
                for t in range(TPB):
                    gather_results(s * TPB + t)

            def normalise(n, first=False):
                pool.wait_ge(inv_landed, n * 64)
                if not first:
                    pool.wait_ge(proj_done, n - 1)
                if not first and not isinstance(n, int):
                    pool.wait_ge(mask_done, (n + 1) * 2 * GROUPS + 2)
                    pool.tensor_tensor(tick[:, 1:2], tick[:, 0:1], tick[:, 0:1], ALU.add)
                pool.tensor_tensor(attn, sums_of[:, bass.ds((n - 1) * 2 * S, 2 * S)], recip, ALU.mult).then_inc(attn_ready, 1)

            for g in range(GROUPS):
                mask_unit(GROUPS + g, g % 2)
                place_values(GROUPS + g + 2, (g + 2) % GROUPS, 1 + (g + 2) // GROUPS)
                for t in range(TPB):
                    gather_results((GROUPS + g) * TPB + t)
            pool.wait_ge(attn_zero, 1)
            mask_unit(2 * GROUPS, 0)
            place_values(2 * GROUPS + 2, 2, 2)
            normalise(1, first=True)
            def add_experts(b):
                j = bass.ds(b * TPB, TPB)
                gates = gate[:, j].unsqueeze(2).to_broadcast([P, TPB, D])
                pool.tensor_tensor(acc[:, j, :], acc[:, j, :], gates, ALU.mult).then_inc(s_scaled, 1)
                pool.wait_ge(s_scaled, b + 1)
                pool.wait_ge(mask_done, ((b + 2) * GROUPS + 2) * 2)
                pool.tensor_tensor(tick[:, 1:2], tick[:, 0:1], tick[:, 0:1], ALU.add)
                pool.tensor_tensor(acc[:, j, :], acc[:, j, :], x_sb[:, j, :], ALU.add).then_inc(s_acc, 1)

            def add_experts_at_end(b):
                j = slice(b * TPB, (b + 1) * TPB)
                gates = gate[:, j].unsqueeze(2).to_broadcast([P, TPB, D])
                pool.tensor_tensor(acc[:, j, :], acc[:, j, :], gates, ALU.mult).then_inc(s_scaled, 1)
                pool.wait_ge(s_scaled, b + 1)
                pool.tensor_tensor(acc[:, j, :], acc[:, j, :], x_sb[:, j, :], ALU.add).then_inc(s_acc, 1)

            pool.wait_ge(s_gath, 16 * TILES)
            pool.wait_ge(s_gate, 1)
            with pool.Fori(2, B - 1) as b:
                for g in (1, 2, 3, 4):
                    mask_unit(b * GROUPS + g, g % 2, normalised=b - 1 if g == 1 else None, added=b - 1 if g == 2 else None)
                    place_values(b * GROUPS + g + 2, (g + 2) % GROUPS, b + (g + 2) // GROUPS)
                    if g == 1:
                        add_experts(b - 2)
                normalise(b)
            for g in (1, 2, 3):
                s = (B - 1) * GROUPS + g
                mask_unit(s, g % 2, normalised=B - 2 if g == 1 else None, added=B - 2 if g == 2 else None)
                if g < 2:
                    place_values(s + 2, g + 2, B - 1)
                    add_experts(B - 3)
                if g == 2:
                    add_experts_at_end(B - 2)
            normalise(B - 1)
            add_experts_at_end(B - 1)

        @block.scalar
        def _(act):
            load_x(act, 1)
            load_x(act, 3)
            act.wait_ge(s_init, 11)
            nc.scalar.activation(lexp[:, 0:1], zeros[:, 0:1], ACT.Sqrt)
            def root(h):
                c = slice(h * TILES // 2, (h + 1) * TILES // 2)
                act.wait_ge(s_var, h + 1)
                nc.scalar.activation(st[:, 3, c], st[:, 2, c], ACT.Sqrt).then_inc(s_root, 1)

            def fourth_rows(h):
                act.wait_ge(s_shift, h + 1)
                for j in range(h * TILES // 2 + 3, (h + 1) * TILES // 2, 4):
                    nc.scalar.activation(xn[:, j, :], x_sb[:, j, :], ACT.Identity, bias=shift[:, j:j + 1],
                                         scale=st[:, 11, j:j + 1]).then_inc(s_xna, 1)

            def copy_xnT(a):
                act.wait_ge(s_xnT, a + 1)
                nc.scalar.activation(xnT[:, a * 512:(a + 1) * 512], p_xnT[a % 2], ACT.Copy).then_inc(s_xnTc, 1)

            def copy_queries(a):
                act.wait_ge(s_in, a + 1)
                src = p_in[a % 4][:, :].rearrange("p (t w) -> p t w", t=2)[:, :, 0:D].rearrange(
                    "p t (g w) -> p g t w", g=GROUPS)
                dst = qk_raw[:, a * 2 * S:(a + 1) * 2 * S].rearrange("p (g k t w) -> p k g t w", g=GROUPS, k=2, t=TPB)[:, 0]
                nc.scalar.activation(dst, src, ACT.Copy, scale=float(HD) ** -0.5).then_inc(s_qc, 1)

            root(0)
            fourth_rows(0)
            copy_xnT(0)
            copy_xnT(1)
            root(1)
            copy_queries(0)
            fourth_rows(1)
            for a in range(1, 4):
                copy_queries(a)
            copy_xnT(2)
            copy_xnT(3)
            for a in range(4, 8):
                copy_queries(a)
            act.wait_ge(s_latsub, 1)
            nc.scalar.activation(lat_sq, l3, ACT.Square).then_inc(s_latsq, 1)
            act.wait_ge(s_latvar, 1)
            nc.scalar.activation(st[:, 8, :], st[:, 7, :], ACT.Sqrt).then_inc(s_latroot, 1)
            act.wait_ge(s_latT, 1)
            nc.scalar.activation(latT[:, :, :].rearrange("p a t -> p (a t)"), p_latT, ACT.Copy).then_inc(s_latTc, 1)
            for j in range(TILES):
                act.wait_ge(s_kv, j + 1)
                src = p_kv[j % 4][:, 0:D].rearrange("p (g w) -> p g w", g=GROUPS)
                dst = qk_raw[:, :].rearrange("p (b g k t w) -> p b k t g w", b=B, g=GROUPS, k=2, t=TPB)[:, j // TPB, 1, j % TPB]
                nc.scalar.activation(dst, src, ACT.Copy).then_inc(s_kc, 1)
            def gelu_tile(t, par):
                act.wait_ge(bias_done, t + 1)
                nc.scalar.activation(hid[par], pre[par], ACT.Gelu).then_inc(gelu_done, 1)

            def expert_slot(t, par, gelu):
                act.wait_ge(hT_done, t + 1)
                nc.scalar.activation(hidT[par], p_hT[par], ACT.Copy).then_inc(hT_copied, 1)
                if gelu:
                    gelu_tile(t + 1, 1 - par)

            def first_parts(b):
                act.wait_ge(s_rotated, b + 1)
                nc.scalar.activation(staged(b, 0), rows_of(b), ACT.Copy).then_inc(s_part1, 1)

            def second_parts(b):
                act.wait_ge(s_left, b + 1)
                nc.scalar.activation(staged(b, 5), rows_of(b), ACT.Copy).then_inc(s_part2, 1)
                for qk, n in ((0, 2), (1, 1)):
                    nc.scalar.activation(of(qk, staged(b, n)), of(qk, rows_of(b)), ACT.Copy).then_inc(s_part2, 1)

            gelu_tile(0, 0)
            for t in (0, 1):
                expert_slot(t, t, True)
            with act.Fori(1, B + 1) as i:
                expert_slot(i * 2, 0, True)
                first_parts(i - 1)
                expert_slot(i * 2 + 1, 1, True)
                second_parts(i - 1)
            for t in range(2 * (B + 1), SLOT_TILES):
                expert_slot(t, t % 2, t + 1 < SLOT_TILES)

            nc.scalar.activation(lexp[:, :], lshift[:, :], ACT.Exp).then_inc(s_lexp, 1)

            def copy_stack(w, g):
                act.wait_ge(stk_done, w + 1)
                nc.scalar.activation(stk_flat(g), p_stk,
                                     ACT.Copy).then_inc(stk_copied, 1)

            def copy_sums(n):
                act.wait_ge(pv_done, n * GROUPS)
                nc.scalar.activation(sums_of[:, bass.ds((n - 1) * 2 * S, 2 * S)], p_o[:, :], ACT.Copy).then_inc(sums_copied, 1)

            def copy_maxima(u, g):
                act.wait_ge(nmT_done, u + 1)
                nc.scalar.activation(nmT[g], p_mb[0:8, 0:S], ACT.Copy).then_inc(nmT_copied, 1)

            def attention_unit(s, g, b, stack, maxima=True):
                if g == 1 and not (isinstance(b, int) and b == 0):
                    copy_sums(b)
                act.wait_ge(st_done, s + 1)
                nc.scalar.activation(probs[g % 2], p_st[:, :], ACT.Exp).then_inc(exp_done, 1)
                if maxima:
                    copy_maxima(s + 2, (g + 2) % GROUPS)
                if stack:
                    copy_stack(s + 4, g)

            def copy_half(i):
                act.wait_ge(pv_done, UNITS - 2 + 2 * i)
                q = slice(i * S, (i + 1) * S)
                nc.scalar.activation(attn_last[:, q], p_o[:, q], ACT.Copy).then_inc(half_copied, 1)

            for b in range(2):
                for g in range(GROUPS):
                    attention_unit(b * GROUPS + g, g, b, True)
            with act.Fori(2, B - 1) as b:
                for g in range(GROUPS):
                    attention_unit(b * GROUPS + g, g, b, True)
            for g in range(GROUPS):
                attention_unit((B - 1) * GROUPS + g, g, B - 1, False, maxima=g < 2)
                if g == 2:
                    copy_half(0)
            copy_half(1)

        @block.vector
        def _(dve):
            v = nc.vector
            steps = [0]

            def step(ins):
                steps[0] += 1
                ins.then_inc(s_dve, 1)
                dve.wait_ge(s_dve, steps[0])

            def bc(ap, n):
                return ap.unsqueeze(2).to_broadcast([P, ap.shape[1], n])

            def ask_root(var, ask_sem, r, c):
                step(v.tensor_scalar(st[:, r, c], var, 1.0, EPS, ALU.mult, ALU.add))
                v.reciprocal(st[:, r + 1, c], st[:, r, c]).then_inc(ask_sem, 1)

            def polish_root(root_sem, n, r, c):
                dve.wait_ge(root_sem, n)
                step(v.tensor_tensor(st[:, 9, c], st[:, r + 2, c], st[:, r + 2, c], ALU.mult))
                step(v.tensor_tensor(st[:, 10, c], st[:, 9, c], st[:, r, c], ALU.mult))
                step(v.tensor_scalar(st[:, 9, c], st[:, 10, c], -0.5, 1.5, ALU.mult, ALU.add))
                step(v.tensor_tensor(st[:, 11, c], st[:, r + 2, c], st[:, 9, c], ALU.mult))

            def statistics(h):
                for j in range(h * TILES // 2, (h + 1) * TILES // 2):
                    if j % 4 == 0:
                        dve.wait_ge(s_x[j // 4], 16)
                    v.bn_stats(out=bn[:, j, :], in_=x_sb[:, j, :]).then_inc(s_bn, 1)
                for j in range(h * TILES // 2, (h + 1) * TILES // 2):
                    dve.wait_ge(s_bn, j + 1)
                    v.bn_aggr(out=mean_var[:, j, :], in_=bn[:, j, :]).then_inc(s_mean, 1)
                c = slice(h * TILES // 2, (h + 1) * TILES // 2)
                dve.wait_ge(s_mean, (h + 1) * TILES // 2)
                ask_root(mean_var[:, c, 1], s_var, 1, c)

            def normalise_rows(h):
                c = slice(h * TILES // 2, (h + 1) * TILES // 2)
                polish_root(s_root, h + 1, 1, c)
                v.scalar_tensor_tensor(shift[:, c], mean_var[:, c, 0], -1.0, st[:, 11, c], ALU.mult, ALU.mult).then_inc(s_shift, 1)
                for j in range(h * TILES // 2, (h + 1) * TILES // 2):
                    if j % 4 != 3:
                        v.tensor_scalar(xn[:, j, :], x_sb[:, j, :], mean_var[:, j, 0:1], st[:, 11, j:j + 1],
                                        ALU.subtract, ALU.mult).then_inc(s_xn, 1)

            statistics(0)
            normalise_rows(0)
            statistics(1)
            normalise_rows(1)

            for a in range(TILES // 2):
                dve.wait_ge(s_in, a + 1)
                src = p_in[a % 4][:, :].rearrange("p (t w) -> p t w", t=2)[:, :, D:QP]
                dve.wait_ge(s_qc, a + 1)
                v.tensor_copy(low[:, 2 * a:2 * a + 2, :], src).then_inc(s_lowc, 1)

            def e3(k):
                return rt[:, k, :].rearrange("p (j e) -> p j e", e=E)

            dve.wait_ge(s_small, 16 * 21)
            dve.wait_ge(s_lowc, TILES // 2)
            dve.wait_ge(s_const, 9)
            row_e = rank_of_e[:, :].unsqueeze(1).to_broadcast([P, TILES, E])
            step(v.tensor_tensor(e3(0), low[:, :, L:L + E], br_all[:, :].unsqueeze(1).to_broadcast([P, TILES, E]), ALU.add))
            step(v.tensor_reduce(st[:, 5, :], e3(0), AX.X, ALU.max))
            step(v.tensor_tensor(e3(1), e3(0), bc(st[:, 5, :], E), ALU.is_equal))
            step(v.tensor_tensor(lshift[:, :].rearrange("p (j e) -> p j e", e=E), e3(0), bc(st[:, 5, :], E), ALU.subtract))
            step(v.tensor_tensor(e3(2), e3(1), row_e, ALU.mult))
            step(v.tensor_reduce(st[:, 1, :], e3(2), AX.X, ALU.max))
            step(v.tensor_tensor(e3(3), row_e, bc(st[:, 1, :], E), ALU.is_equal))
            v.tensor_copy(onehot_b[:, 0:TILES * E], rt[:, 3, :]).then_inc(s_onehot, 1)
            lat = low[:, :, 0:L]
            step(v.tensor_reduce(st[:, 4, :], lat, AX.X, ALU.add))
            v.tensor_scalar(st[:, 0, :], st[:, 4, :], 1.0 / L, None, ALU.mult).then_inc(s_latsum, 1)
            dve.wait_ge(s_rank, 1)
            count = p_route[:, TILES * E:(TILES + 1) * E]
            c3 = cmp[:, 0:E * TILES].rearrange("p (e k) -> p e k", k=TILES)
            step(v.tensor_tensor(c3, bc(count, TILES), mult128[:, :].unsqueeze(1).to_broadcast([P, E, TILES]), ALU.is_gt))
            step(v.tensor_reduce(nte[:, 0, :], c3, AX.X, ALU.add))
            f3 = cmp[:, 0:E * E].rearrange("p (e f) -> p e f", f=E)
            step(v.tensor_tensor(f3, nte[:, 0, :].unsqueeze(1).to_broadcast([P, E, E]), lower[:, :, :], ALU.mult))
            step(v.tensor_reduce(nte[:, 2, :], f3, AX.X, ALU.add))
            step(v.scalar_tensor_tensor(e3(9), nte[:, 2, :].unsqueeze(1).to_broadcast([P, TILES, E]), float(P),
                                        p_route[:, 0:TILES * E].rearrange("p (j e) -> p j e", e=E), ALU.mult, ALU.add))
            step(v.tensor_tensor(e3(10), e3(9), e3(3), ALU.mult))
            step(v.tensor_reduce(slot_f[:, :], e3(10), AX.X, ALU.add))
            v.tensor_copy(slot[:, :], slot_f[:, :]).then_inc(s_slot, 1)
            dve.wait_ge(s_latsq, 1)
            step(v.tensor_reduce(st[:, 4, :], lat_sq, AX.X, ALU.add))
            step(v.tensor_scalar(st[:, 0, :], st[:, 4, :], 1.0 / L, None, ALU.mult))
            ask_root(st[:, 0, :], s_latvar, 6, slice(0, TILES))
            polish_root(s_latroot, 1, 6, slice(0, TILES))
            dve.wait_ge(s_latg, 1)
            step(v.tensor_tensor(lat_g, lat_g, bc(st[:, 11, :], L), ALU.mult))
            v.tensor_tensor(l3, lat_g, beta[:, :].unsqueeze(1).to_broadcast([P, TILES, L]), ALU.add).then_inc(s_latn, 1)
            step(v.tensor_tensor(nte[:, 1, :], nte[:, 2, :], nte[:, 0, :], ALU.add))
            x3 = cmp[:, :].rearrange("p (t e) -> p t e", e=E)
            step(v.tensor_tensor(x3, bc(tile_no[:, :], E), nte[:, 1, :].unsqueeze(1).to_broadcast([P, SLOT_TILES, E]), ALU.is_ge))
            step(v.tensor_reduce(expert_f[:, :], x3, AX.X, ALU.add))
            v.tensor_scalar(expert[:, :], expert_f[:, :], float(E - 1), None, ALU.min).then_inc(s_expert, 1)

            for j in range(TILES):
                dve.wait_ge(s_kv, j + 1)
                dve.wait_ge(s_kc, j + 1)
                v.tensor_copy(v_all[:, j, :], p_kv[j % 4][:, D:2 * D]).then_inc(s_vc, 1)

            def read_scores(u, par, sm=p_sm, before_last=None):
                mv = mx[:, par, :].rearrange("p (t c a) -> p t c a", t=2, c=2)
                t0 = sm[0].rearrange("p (w n) -> p w n", n=P)
                t1 = sm[1].rearrange("p (a n) -> p a n", n=S)
                for k, (dst, src) in enumerate(((mv[:, 1, 0, :], t1), (mx[:, par, 0:4], t0), (mv[:, 1, 1, :], t1))):
                    if k == 2 and before_last is not None:
                        before_last()
                    dve.wait_ge(sm_done, u * 3 + k + 1)
                    v.tensor_reduce(dst, src, AX.X, ALU.max).then_inc(sm_read, 1)
                nv = nm[:, par, :].rearrange("p (t r w) -> p t r w", t=2, r=2)
                m2 = mx[:, par, :].rearrange("p (t w) -> p t w", t=2)
                dve.wait_ge(sm_read, u * 3 + 3)
                v.tensor_scalar(nv[:, :, 0, :], m2, -1.0, None, ALU.mult).then_inc(s_neg, 1)
                dve.wait_ge(s_neg, u + 1)
                v.scalar_tensor_tensor(nv[:, :, 1, :], m2, -1.0, nv[:, :, 0, :], ALU.mult, ALU.subtract).then_inc(nm_ready, 1)

            def copy_maxima(u, g):
                dve.wait_ge(nmT_done, u + 1)
                v.tensor_copy(nmT[g], p_mb[0:8, 0:S]).then_inc(nmT_copied, 1)

            dve.wait_ge(s_bias, 32)
            dve.wait_ge(s_expert, 1)

            def copy_xT(t, par):
                dve.wait_ge(xsT_done, t + 1)
                v.tensor_copy(xsT[par][:, :], p_xsT[:, 0:P]).then_inc(xsT_copied, 1)

            def add_bias(t, par, gelu_before):
                e = nc.vector.value_load(expert[0:1, bass.ds(t, 1)], min_val=0, max_val=E - 1)
                dve.wait_ge(pre_done, t + 1)
                if gelu_before:
                    dve.wait_ge(gelu_done, t - 1)
                v.tensor_tensor(pre[par], p_pre[par], b1_all[:, bass.ds(e * F, F)], ALU.add).then_inc(bias_done, 1)
                return e

            def finish_y(t, par, n_stored, e=None):
                if e is None:
                    e = nc.vector.value_load(expert[0:1, bass.ds(t, 1)], min_val=0, max_val=E - 1)
                dve.wait_ge(y_done, t + 1)
                if n_stored is not None:
                    dve.wait_ge(y_stored[par], n_stored)
                v.tensor_tensor(y_sb[par][:, :], p_y[:, 0:D], b2_all[:, bass.ds(e * D, D)], ALU.add).then_inc(y_copied, 1)

            for t in range(3):
                copy_xT(t, t % 2)
            add_bias(0, 0, False)
            add_bias(1, 1, False)
            for t in (0, 1):
                copy_xT(t + 3, 1 - t)
                add_bias(t + 2, t, True)
                finish_y(t, t, None)
            def copy_stack(w):
                dve.wait_ge(stk_done, w + 1)
                v.tensor_copy(stk_flat(w), p_stk).then_inc(stk_copied, 1)

            def leave_first(b):
                dve.wait_ge(s_part1, b + 1)
                v.tensor_tensor(rows_of(b), rows_of(b), staged(b, 0), ALU.subtract).then_inc(s_left, 1)
                for qk, n in ((0, 1), (0, 3), (1, 2), (1, 4)):
                    v.tensor_copy(of(qk, staged(b, n)), of(qk, staged(b, 0))).then_inc(s_stage, 1)

            def third_parts(b):
                dve.wait_ge(s_part2, b * 3 + 3)
                for qk, n in ((0, 4), (1, 3)):
                    v.tensor_tensor(of(qk, staged(b, n)), of(qk, rows_of(b)), of(qk, staged(b, 5)),
                                    ALU.subtract).then_inc(s_stage, 1)

            with dve.Fori(0, B // 2) as i:
                loaded = [None, None]
                for k in range(4):
                    t = i * 4 + 2 + k
                    copy_xT(t + 3, 1 - k % 2)
                    loaded.append(add_bias(t + 2, k % 2, True))
                    finish_y(t, k % 2, i * 32 + 16 * (1 + k // 2), e=loaded[k])
                    if k % 2 == 0:
                        leave_first(i * 2 + k // 2)
                    else:
                        third_parts(i * 2 + k // 2)
            for t in range(2 * (B + 1), SLOT_TILES):
                if t + 3 < SLOT_TILES:
                    copy_xT(t + 3, 1 - t % 2)
                if t + 2 < SLOT_TILES:
                    add_bias(t + 2, t % 2, True)
                if t < 2 * (B + 1) + GROUPS:
                    copy_stack(t - 2 * (B + 1))
                finish_y(t, t % 2, 16 * (t // 2))
                u = t - (SLOT_TILES - 3)
                if u > 0:
                    copy_maxima(u - 1, u - 1)
                if u >= 0:
                    read_scores(u, u % 2, sm=p_sm_early if u < 2 else p_sm)

            def invert_sums(n):
                dve.wait_ge(den_landed, n * 32)
                v.reciprocal(inv, den).then_inc(inv_ready, 1)

            def normalise_half(i):
                dve.wait_ge(den_done, i + 1)
                q = slice(i * S, (i + 1) * S)
                v.reciprocal(recip_last[:, q], p_den[i]).then_inc(s_rec, 1)
                dve.wait_ge(s_rec, i + 1)
                v.tensor_tensor(attn_last[:, q], attn_last[:, q], recip_last[:, q], ALU.mult).then_inc(half_ready, 1)

            def finish_rows(b, i=0, stored=None, source=p_m):
                dve.wait_ge(s_acc, b + 1)
                dve.wait_ge(proj_done, b + 1)
                if stored is not None:
                    dve.wait_ge(s_out, stored)
                v.tensor_tensor(o_sb[i].rearrange("p (t d) -> p t d", t=TPB),
                                source[:, 0:TPB * D].rearrange("p (t d) -> p t d", t=TPB),
                                acc[:, bass.ds(b * TPB, TPB), :], ALU.add).then_inc(o_ready, 1)

            def attention_unit(s, g, b, scores, sums_too, rows_too):
                def invert():
                    if sums_too and g == 2:
                        invert_sums(b)

                if not scores:
                    invert()
                if rows_too and g == 2:
                    finish_rows(b - 2, stored=None if isinstance(b, int) and b == 2 else (b - 2) * 16)
                if scores:
                    read_scores(s + 3, (g + 1) % 2, before_last=invert)

            dve.wait_ge(s_lexp, 1)
            step(v.tensor_reduce(gsum[:, :], lexp[:, :].rearrange("p (j e) -> p j e", e=E), AX.X, ALU.add))
            v.reciprocal(gate[:, :], gsum[:, :]).then_inc(s_gate, 1)
            v.memset(recip, 0.0).then_inc(attn_zero, 1)
            for b in range(3):
                for g in range(GROUPS):
                    attention_unit(b * GROUPS + g, g, b, True, b > 0, b > 1)
            with dve.Fori(3, B - 1) as b:
                for g in range(GROUPS):
                    attention_unit(b * GROUPS + g, g, b, True, True, True)
            for g in range(GROUPS):
                attention_unit((B - 1) * GROUPS + g, g, B - 1, g == 0, True, True)
            normalise_half(0)
            normalise_half(1)
            finish_rows(B - 2, stored=(B - 2) * 16)
            finish_rows(B - 1, i=1, source=p_last)

        @block.tensor
        def _(pe):
            mm = nc.tensor.matmul
            tr = nc.tensor.transpose
            def transpose_rows(a):
                pe.wait_ge(s_xn, 3 * (a + 1))
                pe.wait_ge(s_xna, a + 1)
                if a >= 2:
                    pe.wait_ge(s_xnTc, a - 1)
                for k in range(4):
                    ins = tr(p_xnT[a % 2][:, k * P:(k + 1) * P], xn[:, 4 * a + k, :], ident[:, :])
                ins.then_inc(s_xnT, 1)

            def first_product(a):
                pe.wait_ge(s_xnTc, a // 2 + 1)
                if a >= 4:
                    pe.wait_ge(s_qc, a - 3)
                    pe.wait_ge(s_lowc, a - 3)
                for t in range(2):
                    j = 2 * a + t
                    ins = mm(p_in[a % 4][:, t * 256:t * 256 + QP], xnT[:, j * P:(j + 1) * P], w_in[:, :], start=True, stop=True)
                ins.then_inc(s_in, 1)

            pe.wait_ge(s_const, 9)
            transpose_rows(0)
            transpose_rows(1)
            pe.wait_ge(s_win, 48)
            for a in range(4):
                first_product(a)
            transpose_rows(2)
            transpose_rows(3)
            for a in range(4, 8):
                first_product(a)
            pe.wait_ge(s_onehot, 1)
            n = (TILES + 1) * E
            mm(p_route[:, 0:n], before[:, :], onehot_b[:, :], start=True, stop=False, skip_group_check=True)
            for j in range(TILES):
                ins = mm(p_route[:, (j + 1) * E:n].rearrange("p (k e) -> p k e", e=E), ones_b[:, :],
                         onehot_b[:, j * E:(j + 1) * E].unsqueeze(1).to_broadcast([P, TILES - j, E]),
                         start=False, stop=(j == TILES - 1), skip_group_check=True)
            ins.then_inc(s_rank, 1)
            pe.wait_ge(s_latn, 1)
            for a in range(4):
                ins = tr(p_latT[:, a * P:(a + 1) * P], latn[:, a * P:(a + 1) * P], ident[:, :])
            ins.then_inc(s_latT, 1)
            pe.wait_ge(s_latTc, 1)
            pe.wait_ge(s_small, 16 * 21)
            pe.wait_ge(s_qc, TILES // 2)
            pe.wait_ge(s_lowc, TILES // 2)
            for j in range(TILES):
                if j >= 4:
                    pe.wait_ge(s_vc, j - 3)
                r = slice(L * (j % 4), L * (j % 4 + 1))
                mm(p_kv[j % 4][:, 0:2 * D], latT[r, j // 4, :], w_kv[r, :], start=True, stop=True).then_inc(s_kv, 1)

            def rows_T(t, par, loaded, copied):
                pe.wait_ge(xs_loaded[par], loaded)
                if copied is not None:
                    pe.wait_ge(xsT_copied, copied)
                tr(p_xsT[:, 0:P], xs[par][:, :], ident[:, :]).then_inc(xsT_done, 1)

            def first_half(t, par, biased):
                e = nc.tensor.value_load(expert[0:1, bass.ds(t, 1)], min_val=0, max_val=E - 1)
                pe.wait_ge(xsT_copied, t + 1)
                if biased is not None:
                    pe.wait_ge(bias_done, biased)
                mm(p_pre[par], xsT[par][:, :], w1[:, bass.ds(e * F, F)], start=True, stop=True).then_inc(pre_done, 1)
                return e

            def hidden_T(t, par, copied):
                pe.wait_ge(gelu_done, t + 1)
                if copied is not None:
                    pe.wait_ge(hT_copied, copied)
                for c in range(FC):
                    ins = tr(p_hT[par][:, c * P:(c + 1) * P], hid[par][:, c * P:(c + 1) * P], ident[:, :])
                ins.then_inc(hT_done, 1)

            def second_half(t, par, copied, e=None):
                if e is None:
                    e = nc.tensor.value_load(expert[0:1, bass.ds(t, 1)], min_val=0, max_val=E - 1)
                pe.wait_ge(hT_copied, t + 1)
                if copied is not None:
                    pe.wait_ge(y_copied, copied)
                for c in range(FC):
                    ins = mm(p_y[:, 0:D], hidT[par][:, c * P:(c + 1) * P], w2[:, bass.ds(e * (FC * D) + c * D, D)],
                             start=(c == 0), stop=(c == FC - 1))
                ins.then_inc(y_done, 1)

            def stack(w, g, first=False, steps=range(8)):
                if not first and steps[0] == 0:
                    pe.wait_ge(stk_copied, w)
                unit = stage[:, bass.ds(w * CH, CH)]
                for i in steps:
                    lo = ((i // 4 * TPB + i % 2) * G + 2 * (i // 2 % 2)) * HW
                    ins = tr(p_stk[:, i * P:(i + 1) * P], unit[:, lo:lo + 2 * HW], ident_b[:, :])
                if steps[-1] == 7:
                    ins.then_inc(stk_done, 1)


            def mask(bk):
                mm(bk, ident_b[:, :], causal_neg[:, :].unsqueeze(1).to_broadcast([P, bk.shape[1], P]),
                   start=True, stop=False, skip_group_check=True)

            def by_query_tile0(g, c, sm):
                for a in range(2):
                    to = (2 * c + a) * P
                    ins = mm(sm[0][:, to:to + P], q_rows(g, c, a, 0, P, ROWS), k_rows(g, c, a, 0, ROWS),
                             start=False, stop=(c == 1 and a == 1), skip_group_check=True)
                return ins

            def by_query_tile1(g, c, sm):
                mask(sm[1].rearrange("p (a n) -> p a n", a=2)[:, :, P:S])
                for a in range(2):
                    ins = mm(sm[1][:, a * S:(a + 1) * S], q_rows(g, c, a, P, S, ROWS),
                             stk[g][64 * c:64 * c + ROWS, 1, a, 0:S], start=False, stop=(a == 1), skip_group_check=True)
                ins.then_inc(sm_done, 1)

            def scores_by_query(u, g, first=False, sm=p_sm, stack_too=False):
                pe.wait_ge(stk_copied, u + 1)
                if not first:
                    pe.wait_ge(sm_read, u * 3 - 1)
                mask(sm[0].rearrange("p (w n) -> p w n", w=G))
                by_query_tile0(g, 0, sm).then_inc(sm_half, 1)
                if stack_too:
                    stack(u + 1, (g + 1) % GROUPS, steps=range(0, 2))
                if not first:
                    pe.wait_ge(sm_read, u * 3)
                by_query_tile1(g, 0, sm)
                if stack_too:
                    stack(u + 1, (g + 1) % GROUPS, steps=range(2, 5))
                pe.wait_ge(sm_half, u + 1)
                by_query_tile0(g, 1, sm).then_inc(sm_done, 1)
                if stack_too:
                    stack(u + 1, (g + 1) % GROUPS, steps=range(5, 8))

            def scores_by_query_rest(u, g, sm=p_sm):
                pe.wait_ge(sm_read, u * 3 + 1)
                by_query_tile1(g, 1, sm)

            def maxima_T(u, par):
                pe.wait_ge(nm_ready, u + 1)
                for t in range(TPB):
                    ins = tr(p_mb[0:8, t * P:(t + 1) * P], nm[:, par, 8 * t:8 * t + 8], ident_b[:, :])
                ins.then_inc(nmT_done, 1)

            pe.wait_ge(s_expert, 1)
            pe.wait_ge(s_vc, TILES)
            rows_T(0, 0, 16, None)
            rows_T(1, 1, 16, 1)
            pe.wait_ge(s_w1, 16)
            first_half(0, 0, None)
            rows_T(2, 0, 32, 2)
            first_half(1, 1, None)
            pe.wait_ge(s_w2, 16)
            for t in (0, 1):
                hidden_T(t, t, None)
                rows_T(t + 3, 1 - t, 32 + 16 * t, t + 3)
                first_half(t + 2, t, t + 1)
                second_half(t, t, None if t == 0 else 1)
            with pe.Fori(0, B // 2) as i:
                loaded = [None, None]
                for k in range(4):
                    t, par = i * 4 + 2 + k, k % 2
                    hidden_T(t, par, t - 1)
                    rows_T(t + 3, 1 - par, i * 32 + 16 * ((5 + k) // 2 + 1), t + 3)
                    loaded.append(first_half(t + 2, par, t + 1))
                    second_half(t, par, t, e=loaded[k])
            for t in range(2 * (B + 1), SLOT_TILES):
                w = t - 2 * (B + 1)
                u = t - (SLOT_TILES - 3)
                hidden_T(t, t % 2, t - 1)
                if u > 0:
                    scores_by_query_rest(u - 1, u - 1, sm=p_sm_early)
                if t + 3 < SLOT_TILES:
                    rows_T(t + 3, (t + 3) % 2, 16 * ((t + 3) // 2 + 1), t + 3)
                if t + 2 < SLOT_TILES:
                    first_half(t + 2, t % 2, t + 1)
                if w == 0:
                    pe.wait_ge(s_stage, 6)
                    pe.wait_ge(s_rows, 3)
                if w < GROUPS:
                    stack(w, w, first=(w == 0))
                second_half(t, t % 2, t)
                if u > 0:
                    if u > 1:
                        pe.wait_ge(nmT_copied, u - 1)
                    maxima_T(u - 1, u - 1)
                if u == 0:
                    pe.wait_ge(xsT_copied, SLOT_TILES)
                    pe.wait_ge(bias_done, SLOT_TILES - 1)
                if u >= 0:
                    scores_by_query(u, u, first=(u == 0), sm=p_sm_early if u < 2 else p_sm)
            scores_by_query_rest(2, 2)

            def scores_by_key(s, g, landed, first=False):
                pe.wait_ge(m_landed[g], landed)
                if not first:
                    pe.wait_ge(exp_done, s)
                for c in range(2):
                    for a in range(2):
                        to = (2 * c + a) * S
                        mm(p_st[:, to:to + S], k_rows(g, c, a, 0, SH), q_rows(g, c, a, 0, S, SH), start=True, stop=True)
                    if c == 1:
                        pe.wait_ge(st_half, s + 1)
                    for a in range(2):
                        to = G * S + (2 * c + a) * P
                        ins = mm(p_st[:, to:to + P], k_rows(g, c, a, 1, SH), q_rows(g, c, a, P, S, SH), start=True, stop=True)
                    ins.then_inc(st_done if c else st_half, 1)

            def weigh_values(s, g):
                pe.wait_ge(mask_done, s * 2 + 2)
                pe.wait_ge(v_placed, s + 1)
                q = S * (g // 2)
                for t in range(TPB):
                    lo, n = (0, S) if t == 0 else (G * S, P)
                    for a in range(2):
                        for c in range(2):
                            r, h, k = 64 * (g % 2) + 32 * c, 2 * a + c, 2 * c + a
                            ins = mm(p_o[r:r + 32, q + S - n:q + S], v_pad[g][:, (t * G + h) * VW:(t * G + h + 1) * VW],
                                     probs[g % 2][:, lo + k * n:lo + (k + 1) * n],
                                     start=(t == 0 and a == 0), stop=(t == 1 and a == 1))
                ins.then_inc(pv_done, 1)

            def project(rows, to=p_m):
                for t in range(TPB):
                    for i in range(2):
                        ins = mm(to[:, t * D:(t + 1) * D], rows[:, i * S + t * P:i * S + (t + 1) * P], w_o[:, i, :],
                                 start=(i == 0), stop=(i == 1))
                ins.then_inc(proj_done, 1)

            def spread_den(i):
                pe.wait_ge(half_copied, i + 1)
                if i == 1:
                    pe.wait_ge(sm_read, UNITS * 3)
                mm(p_den[i], den_rows[:, :], attn_last[:, i * S:(i + 1) * S], start=True, stop=True).then_inc(den_done, 1)

            def attention_unit(s, g, b, more_stack, more_scores, more_maxima, sums_too, rows_too):
                scores_by_key(s, g, (b + 1) * 32, first=not sums_too and g == 0)
                if more_scores:
                    scores_by_query(s + 3, (g + 3) % GROUPS, stack_too=more_stack)
                if more_maxima:
                    if g == 2 and rows_too:
                        pe.wait_ge(o_ready, b - 1)
                    else:
                        pe.wait_ge(nmT_copied, s + 2)
                    maxima_T(s + 2, g % 2)
                if sums_too or g > 0:
                    if g == 1 and sums_too:
                        pe.wait_ge(sums_copied, b)
                    if g == 3 and not more_stack:
                        spread_den(0)
                    weigh_values(s - 1, (g + 3) % GROUPS)
                if rows_too and g == 1:
                    pe.wait_ge(nmT_copied, s + 3)
                    pe.wait_ge(attn_ready, b - 1)
                    project(attn)
                if more_scores:
                    scores_by_query_rest(s + 3, (g + 3) % GROUPS)

            pe.wait_ge(y_copied, SLOT_TILES)
            pe.wait_ge(s_stage, B * 6)
            pe.wait_ge(bias_done, SLOT_TILES)
            for b in range(2):
                for g in range(GROUPS):
                    attention_unit(b * GROUPS + g, g, b, True, True, True, b > 0, b > 1)
            with pe.Fori(2, B - 1) as b:
                for g in range(GROUPS):
                    attention_unit(b * GROUPS + g, g, b, True, True, True, True, True)
            for g in range(GROUPS):
                attention_unit((B - 1) * GROUPS + g, g, B - 1, False, g == 0, g < 2, True, True)
            weigh_values(UNITS - 1, GROUPS - 1)
            spread_den(1)
            pe.wait_ge(o_ready, B - 2)
            pe.wait_ge(attn_ready, B - 1)
            project(attn)
            pe.wait_ge(half_ready, 2)
            project(attn_last, to=p_last)


_IN = ["x", "W_q", "W_dkv", "W_uk", "W_uv", "W_o", "ln_gamma", "ln_beta", "W1", "b1", "W2", "b2", "Wr", "br", "cos", "sin"]


def kernel(L0_attn_x, L0_attn_W_q, L0_attn_W_dkv, L0_attn_W_uk, L0_attn_W_uv, L0_attn_W_o, L0_attn_ln_gamma,
           L0_attn_ln_beta, L0_ffn_W1, L0_ffn_b1, L0_ffn_W2, L0_ffn_b2, L0_ffn_Wr, L0_ffn_br):
    import numpy as np
    import concourse.bacc as bacc
    from concourse.bass_utils import run_bass_kernel_spmd

    half = HD // 2
    inv_freq = (np.float32(1.0) / np.power(np.float32(10000.0), np.arange(half, dtype=np.float32) / np.float32(half))).astype(np.float32)
    angle = (np.arange(S, dtype=np.float32)[:, None] * inv_freq[None, :]).astype(np.float32)
    cos = np.concatenate([np.cos(angle)] * 2, axis=1).astype(np.float32)
    sin = np.concatenate([-np.sin(angle), np.sin(angle)], axis=1).astype(np.float32)

    def table(t):
        t = t.reshape(TPB, P, 1, HD).transpose(1, 0, 2, 3)
        return np.ascontiguousarray(np.broadcast_to(t, (P, TPB, G, HD)).reshape(P, TPB * G * HD))

    values = [L0_attn_x, L0_attn_W_q, L0_attn_W_dkv, L0_attn_W_uk, L0_attn_W_uv, L0_attn_W_o, L0_attn_ln_gamma,
              L0_attn_ln_beta, L0_ffn_W1, L0_ffn_b1, L0_ffn_W2, L0_ffn_b2, L0_ffn_Wr, L0_ffn_br, table(cos), table(sin)]
    nc = bacc.Bacc("TRN2", target_bir_lowering=False, num_devices=1)
    arrays, args = {}, []
    for name, value in zip(_IN, values):
        a = np.ascontiguousarray(value)
        arrays[f"in_{name}"] = a
        args.append(nc.dram_tensor(f"in_{name}", a.shape, mybir.dt.from_np(a.dtype), kind="ExternalInput").ap())
    out = nc.dram_tensor("out_rows", (B, S, D), F32, kind="ExternalOutput").ap()
    layer_program(nc, *args, out)
    r = run_bass_kernel_spmd(nc, [arrays], core_ids=[0])
    return r.results[0]["out_rows"]
```
